# Optimizing a Trainium2 kernel written in Bass

```python
import numpy as np
import jax
import jax.numpy as jnp

def _softmax(x, axis=-1):
    return jax.nn.softmax(x, axis=axis)

def _gelu(x):
    return jax.nn.gelu(x, approximate=True)

def _silu(x):
    return jax.nn.silu(x)

def _sigmoid(x):
    return jax.nn.sigmoid(x)

def _layernorm(x, axis=-1, eps=1e-05):
    m = jnp.mean(x, axis=axis, keepdims=True)
    v = jnp.var(x, axis=axis, keepdims=True)
    return (x - m) / jnp.sqrt(v + eps)

def _scatter_add(tgt, idx, src, axis=0):
    return tgt.at[idx].add(src)

def _segment_sum(src, seg, n):
    return jax.ops.segment_sum(src, seg, n)
kernel_name = 'mk_sandwich_d1_jaxref_r4_9164ea'

def setup_inputs(seed: int=0):
    np.random.seed(seed)
    _w = jnp.asarray

    def _L0_attn_setup():
        import jax, jax.numpy as jnp
        import numpy as np
        import math
        D = 512
        NH = 16
        HD = D // NH

        def rotary_apply(x, cos, sin):
            d = x.shape[-1]
            x1, x2 = (x[..., :d // 2], x[..., d // 2:])
            c, s = (cos[..., :d // 2], sin[..., :d // 2])
            return jnp.concatenate([x1 * c - x2 * s, x2 * c + x1 * s], axis=-1)
        key = jax.random.key(seed)
        k1, k2, k3 = jax.random.split(key, 3)
        x = jax.random.normal(k1, (2, 512, D), dtype=jnp.float32)
        w_qkv = jax.random.normal(k2, (D, 3 * D), dtype=jnp.float32) * (1.0 / math.sqrt(D))
        w_o = jax.random.normal(k3, (D, D), dtype=jnp.float32) * (1.0 / math.sqrt(D))
        return {'x': x, 'w_qkv': w_qkv, 'w_o': w_o}
    _L0_attn_in = _L0_attn_setup()

    def _L0_ffn_setup():
        import jax, jax.numpy as jnp
        import numpy as np
        B, S, H = (4, 256, 512)
        NH = 16
        HD = H // NH
        RD = HD // 2
        LAT = H // 4
        I = 256
        NE = 8
        NSH = 1
        NR = NE - NSH
        TOPK = 2
        EPS = 1e-05
        SCALING = 8.0

        def _w(key, shape, fan_in):
            return jax.random.normal(key, shape, dtype=jnp.float32) / np.sqrt(fan_in)

        def rmsnorm(x, w):
            rms = jax.lax.rsqrt(jnp.mean(x * x, axis=-1, keepdims=True) + EPS)
            return w * rms * x

        def rope_cos_sin(seq_len):
            inv_freq = 1.0 / 10000.0 ** (jnp.arange(0, RD, 2, dtype=jnp.float32) / RD)
            t = jnp.arange(seq_len, dtype=jnp.float32)
            ang = jnp.outer(t, inv_freq)
            emb = jnp.concatenate([ang, ang], axis=-1)
            return (jnp.cos(emb), jnp.sin(emb))

        def apply_rope(x, cos, sin):
            c = cos[None, :, None, :]
            s = sin[None, :, None, :]
            x1, x2 = jnp.split(x, 2, axis=-1)
            rot = jnp.concatenate([-x2, x1], axis=-1)
            return x * c + rot * s

        def expert_ffn(x, wg, wu, wd):
            h = jax.nn.silu(x @ wg) * (x @ wu) / SCALING
            return h @ wd

        def attention(x, kv_d_w, q_d_w, k_u_w, v_u_w, q_u_w, rope_k_w, rope_q_w, o_w):
            b, s, _ = x.shape
            kv_d = x @ kv_d_w
            q_d = x @ q_d_w
            k_p = (kv_d @ k_u_w).reshape(b, s, NH, RD)
            q_p = (q_d @ q_u_w).reshape(b, s, NH, RD)
            v = (kv_d @ v_u_w).reshape(b, s, NH, HD)
            k_r = (x @ rope_k_w).reshape(b, s, NH, RD)
            q_r = (q_d @ rope_q_w).reshape(b, s, NH, RD)
            cos, sin = rope_cos_sin(s)
            k_r = apply_rope(k_r, cos, sin)
            q_r = apply_rope(q_r, cos, sin)
            k = jnp.concatenate([k_p, k_r], axis=-1)
            q = jnp.concatenate([q_p, q_r], axis=-1)
            scale = 1.0 / np.sqrt(HD)
            scores = jnp.einsum('bqhd,bkhd->bhqk', q, k) * scale
            causal = jnp.tril(jnp.ones((s, s), dtype=bool))
            scores = jnp.where(causal[None, None], scores, jnp.finfo(scores.dtype).min)
            probs = jax.nn.softmax(scores, axis=-1)
            out = jnp.einsum('bhqk,bkhd->bqhd', probs, v).reshape(b, s, H)
            return out @ o_w

        def moe(x, sh_gate, sh_up, sh_down, r_gate, r_up, r_down, router_w, router_b):
            shared = expert_ffn(x, sh_gate, sh_up, sh_down)
            logits = x @ router_w + router_b
            probs = jax.nn.sigmoid(logits)
            scores, idx = jax.lax.top_k(probs, TOPK)
            scores = scores / jnp.sum(scores, axis=-1, keepdims=True)
            w = jnp.sum(jax.nn.one_hot(idx, NR, dtype=x.dtype) * scores[..., None], axis=-2)
            combined = jnp.zeros_like(x)
            for e in range(NR):
                combined = combined + w[..., e:e + 1] * expert_ffn(x, r_gate[e], r_up[e], r_down[e])
            return shared + combined
        key = jax.random.key(seed)
        ks = jax.random.split(key, 24)
        return {'x': jax.random.normal(ks[0], (B, S, H), dtype=jnp.float32), 'ln1_w': jnp.ones((H,), jnp.float32), 'ln2_w': jnp.ones((H,), jnp.float32), 'kv_d_w': _w(ks[1], (H, LAT), H), 'q_d_w': _w(ks[2], (H, LAT), H), 'k_u_w': _w(ks[3], (LAT, H // 2), LAT), 'v_u_w': _w(ks[4], (LAT, H), LAT), 'q_u_w': _w(ks[5], (LAT, H // 2), LAT), 'rope_k_w': _w(ks[6], (H, H // 2), H), 'rope_q_w': _w(ks[7], (LAT, H // 2), LAT), 'o_w': _w(ks[8], (H, H), H), 'sh_gate': _w(ks[9], (H, I), H), 'sh_up': _w(ks[10], (H, I), H), 'sh_down': _w(ks[11], (I, H), I), 'r_gate': _w(ks[12], (NR, H, I), H), 'r_up': _w(ks[13], (NR, H, I), H), 'r_down': _w(ks[14], (NR, I, H), I), 'router_w': _w(ks[15], (H, NR), H), 'router_b': jnp.zeros((NR,), jnp.float32)}
    _L0_ffn_in = _L0_ffn_setup()
    _d = {'L0_attn_x': _L0_attn_in['x'], 'L0_attn_w_qkv': _L0_attn_in['w_qkv'], 'L0_attn_w_o': _L0_attn_in['w_o'], 'L0_ffn_ln1_w': _L0_ffn_in['ln1_w'], 'L0_ffn_ln2_w': _L0_ffn_in['ln2_w'], 'L0_ffn_kv_d_w': _L0_ffn_in['kv_d_w'], 'L0_ffn_q_d_w': _L0_ffn_in['q_d_w'], 'L0_ffn_k_u_w': _L0_ffn_in['k_u_w'], 'L0_ffn_v_u_w': _L0_ffn_in['v_u_w'], 'L0_ffn_q_u_w': _L0_ffn_in['q_u_w'], 'L0_ffn_rope_k_w': _L0_ffn_in['rope_k_w'], 'L0_ffn_rope_q_w': _L0_ffn_in['rope_q_w'], 'L0_ffn_o_w': _L0_ffn_in['o_w'], 'L0_ffn_sh_gate': _L0_ffn_in['sh_gate'], 'L0_ffn_sh_up': _L0_ffn_in['sh_up'], 'L0_ffn_sh_down': _L0_ffn_in['sh_down'], 'L0_ffn_r_gate': _L0_ffn_in['r_gate'], 'L0_ffn_r_up': _L0_ffn_in['r_up'], 'L0_ffn_r_down': _L0_ffn_in['r_down'], 'L0_ffn_router_w': _L0_ffn_in['router_w'], 'L0_ffn_router_b': _L0_ffn_in['router_b']}
    _x0 = _d['L0_attn_x']
    _d['L0_attn_x'] = jax.random.normal(jax.random.fold_in(jax.random.key(seed), 1), (8, 512, 512), dtype=_x0.dtype)
    del _x0
    return _d

def reference(L0_attn_x, L0_attn_w_qkv, L0_attn_w_o, L0_ffn_ln1_w, L0_ffn_ln2_w, L0_ffn_kv_d_w, L0_ffn_q_d_w, L0_ffn_k_u_w, L0_ffn_v_u_w, L0_ffn_q_u_w, L0_ffn_rope_k_w, L0_ffn_rope_q_w, L0_ffn_o_w, L0_ffn_sh_gate, L0_ffn_sh_up, L0_ffn_sh_down, L0_ffn_r_gate, L0_ffn_r_up, L0_ffn_r_down, L0_ffn_router_w, L0_ffn_router_b):

    def _L0_attn_ref(x, w_qkv, w_o):
        import jax, jax.numpy as jnp
        import numpy as np
        import math
        D = 512
        NH = 16
        HD = D // NH

        def rotary_apply(x, cos, sin):
            d = x.shape[-1]
            x1, x2 = (x[..., :d // 2], x[..., d // 2:])
            c, s = (cos[..., :d // 2], sin[..., :d // 2])
            return jnp.concatenate([x1 * c - x2 * s, x2 * c + x1 * s], axis=-1)
        B, T, _ = x.shape
        qkv = (x @ w_qkv).reshape(B, T, 3, NH, HD)
        q, k, v = (qkv[:, :, 0], qkv[:, :, 1], qkv[:, :, 2])
        inv_freq = 1.0 / 10000.0 ** (jnp.arange(0, HD, 2, dtype=jnp.float32) / HD)
        t = jnp.arange(T, dtype=jnp.float32)
        freqs = jnp.outer(t, inv_freq)
        emb = jnp.concatenate([freqs, freqs], axis=-1)
        cos = jnp.cos(emb)[None, None]
        sin = jnp.sin(emb)[None, None]
        q = rotary_apply(jnp.transpose(q, (0, 2, 1, 3)), cos, sin)
        k = rotary_apply(jnp.transpose(k, (0, 2, 1, 3)), cos, sin)
        v = jnp.transpose(v, (0, 2, 1, 3))
        scores = jnp.einsum('bhqd,bhkd->bhqk', q, k) / math.sqrt(HD)
        causal = jnp.tril(jnp.ones((T, T), dtype=bool))
        scores = jnp.where(causal, scores, -jnp.inf)
        attn = jax.nn.softmax(scores, axis=-1)
        out = jnp.einsum('bhqk,bhkd->bhqd', attn, v)
        out = jnp.transpose(out, (0, 2, 1, 3)).reshape(B, T, D)
        return out @ w_o

    def _L0_ffn_ref(x, ln1_w, ln2_w, kv_d_w, q_d_w, k_u_w, v_u_w, q_u_w, rope_k_w, rope_q_w, o_w, sh_gate, sh_up, sh_down, r_gate, r_up, r_down, router_w, router_b):
        import jax, jax.numpy as jnp
        import numpy as np
        B, S, H = (4, 256, 512)
        NH = 16
        HD = H // NH
        RD = HD // 2
        LAT = H // 4
        I = 256
        NE = 8
        NSH = 1
        NR = NE - NSH
        TOPK = 2
        EPS = 1e-05
        SCALING = 8.0

        def _w(key, shape, fan_in):
            return jax.random.normal(key, shape, dtype=jnp.float32) / np.sqrt(fan_in)

        def rmsnorm(x, w):
            rms = jax.lax.rsqrt(jnp.mean(x * x, axis=-1, keepdims=True) + EPS)
            return w * rms * x

        def rope_cos_sin(seq_len):
            inv_freq = 1.0 / 10000.0 ** (jnp.arange(0, RD, 2, dtype=jnp.float32) / RD)
            t = jnp.arange(seq_len, dtype=jnp.float32)
            ang = jnp.outer(t, inv_freq)
            emb = jnp.concatenate([ang, ang], axis=-1)
            return (jnp.cos(emb), jnp.sin(emb))

        def apply_rope(x, cos, sin):
            c = cos[None, :, None, :]
            s = sin[None, :, None, :]
            x1, x2 = jnp.split(x, 2, axis=-1)
            rot = jnp.concatenate([-x2, x1], axis=-1)
            return x * c + rot * s

        def expert_ffn(x, wg, wu, wd):
            h = jax.nn.silu(x @ wg) * (x @ wu) / SCALING
            return h @ wd

        def attention(x, kv_d_w, q_d_w, k_u_w, v_u_w, q_u_w, rope_k_w, rope_q_w, o_w):
            b, s, _ = x.shape
            kv_d = x @ kv_d_w
            q_d = x @ q_d_w
            k_p = (kv_d @ k_u_w).reshape(b, s, NH, RD)
            q_p = (q_d @ q_u_w).reshape(b, s, NH, RD)
            v = (kv_d @ v_u_w).reshape(b, s, NH, HD)
            k_r = (x @ rope_k_w).reshape(b, s, NH, RD)
            q_r = (q_d @ rope_q_w).reshape(b, s, NH, RD)
            cos, sin = rope_cos_sin(s)
            k_r = apply_rope(k_r, cos, sin)
            q_r = apply_rope(q_r, cos, sin)
            k = jnp.concatenate([k_p, k_r], axis=-1)
            q = jnp.concatenate([q_p, q_r], axis=-1)
            scale = 1.0 / np.sqrt(HD)
            scores = jnp.einsum('bqhd,bkhd->bhqk', q, k) * scale
            causal = jnp.tril(jnp.ones((s, s), dtype=bool))
            scores = jnp.where(causal[None, None], scores, jnp.finfo(scores.dtype).min)
            probs = jax.nn.softmax(scores, axis=-1)
            out = jnp.einsum('bhqk,bkhd->bqhd', probs, v).reshape(b, s, H)
            return out @ o_w

        def moe(x, sh_gate, sh_up, sh_down, r_gate, r_up, r_down, router_w, router_b):
            shared = expert_ffn(x, sh_gate, sh_up, sh_down)
            logits = x @ router_w + router_b
            probs = jax.nn.sigmoid(logits)
            scores, idx = jax.lax.top_k(probs, TOPK)
            scores = scores / jnp.sum(scores, axis=-1, keepdims=True)
            w = jnp.sum(jax.nn.one_hot(idx, NR, dtype=x.dtype) * scores[..., None], axis=-2)
            combined = jnp.zeros_like(x)
            for e in range(NR):
                combined = combined + w[..., e:e + 1] * expert_ffn(x, r_gate[e], r_up[e], r_down[e])
            return shared + combined
        h = x + attention(rmsnorm(x, ln1_w), kv_d_w, q_d_w, k_u_w, v_u_w, q_u_w, rope_k_w, rope_q_w, o_w)
        out = h + moe(rmsnorm(h, ln2_w), sh_gate, sh_up, sh_down, r_gate, r_up, r_down, router_w, router_b)
        return out
    x = L0_attn_x
    x = x + _layernorm(_L0_attn_ref(_layernorm(x, axis=-1), L0_attn_w_qkv, L0_attn_w_o), axis=-1)
    x = x + _layernorm(_L0_ffn_ref(_layernorm(x, axis=-1), L0_ffn_ln1_w, L0_ffn_ln2_w, L0_ffn_kv_d_w, L0_ffn_q_d_w, L0_ffn_k_u_w, L0_ffn_v_u_w, L0_ffn_q_u_w, L0_ffn_rope_k_w, L0_ffn_rope_q_w, L0_ffn_o_w, L0_ffn_sh_gate, L0_ffn_sh_up, L0_ffn_sh_down, L0_ffn_r_gate, L0_ffn_r_up, L0_ffn_r_down, L0_ffn_router_w, L0_ffn_router_b), axis=-1)
    return x

_drawn_inputs = setup_inputs


def setup_inputs(seed=0):
    import zlib

    import numpy as np

    out = dict(_drawn_inputs(seed))
    spreads = {'L0_ffn_ln1_w': (1.0, 0.2), 'L0_ffn_ln2_w': (1.0, 0.6), 'L0_ffn_router_b': (0.0, 0.8)}
    factors = {'L0_ffn_r_gate': 2.674, 'L0_ffn_router_w': 2.871}
    for name, (base, spread) in spreads.items():
        noise = np.random.default_rng([zlib.crc32(name.encode()), seed]).standard_normal(out[name].shape)
        drawn = base * np.exp(spread * noise) if base else spread * noise
        out[name] = jnp.asarray(drawn.astype(out[name].dtype))
    for name, factor in factors.items():
        out[name] = (out[name] * factor).astype(out[name].dtype)
    return out
```

```python
from contextlib import ExitStack

import numpy as np

import concourse.bass as bass
from concourse import mybir

F32 = mybir.dt.float32
F32R = mybir.dt.float32r
BF16 = mybir.dt.bfloat16
U32 = mybir.dt.uint32
ALU = mybir.AluOpType
ACT = mybir.ActivationFunctionType

P = 128
D = 512
CT = D // P
T = 512
TT = T // P
NH = 16
HD = D // NH
GH = P // HD
NG = NH // GH
RD = HD // 2
LAT = D // 4
FF = 256
FT = FF // P
NR = 7
NE = NR + 1
EPS = 1e-5
SCALE = float(HD) ** -0.5
MASKED = -3.0e38
ROWMAX = 3 * HD
STACKS = 3


class Signal:

    def __init__(self, sem, per_pass):
        self.sem, self.per_pass = sem, per_pass

    def after(self, i, k):
        return self.sem, i * self.per_pass + (k + 1)


class Banks:

    def __init__(self, tensor, filled, freed, names):
        self.tensor, self.filled, self.freed = tensor, filled, freed
        self.n = len(freed)
        assert len(names) % self.n == 0 and len(set(names)) == len(names)
        self.number = {name: k for k, name in enumerate(names)}
        self.per_pass = len(names)

    def at(self, name):
        return self.number[name] % self.n

    def bank(self, name):
        return self.tensor[:, self.at(name), :]

    def full(self, i, name):
        return self.filled, i * self.per_pass + (self.number[name] + 2)

    def empty(self, i, name):
        return self.freed[self.at(name)], i * (self.per_pass // self.n) + (self.number[name] // self.n + 1)

    def out(self, i, name):
        return self.freed[self.at(name)], i * (self.per_pass // self.n) + (self.number[name] // self.n + 2)

    def release(self, name):
        return self.freed[self.at(name)]


def attention_order(a):
    heads_in = {0: [0], 1: [1], 2: [2, 3], 3: []}
    yield "qkT", 0, 0
    for h in range(GH):
        yield "S", 0, h
    yield "qkT", 1, 0
    yield "mT", 0, 0
    for g in range(NG):
        for j in range(TT):
            yield "ST", g, j
            if g + 1 < NG:
                for h in heads_in[j]:
                    yield "S", g + 1, h
            if j == TT - 1 and g + 2 < NG:
                yield "qkT", g + 2, 0
            if j > 0:
                yield "PV", g, j - 1
        if g + 1 < NG:
            yield "mT", g + 1, 0
        yield "PV", g, TT - 1


def attention_fills(a):
    for step, g, h in attention_order(a):
        if step == "qkT":
            yield from [("qT", a, g), ("kT", a, g)]
        if step == "S":
            yield from [("S", a, g, h, part) for part in range(3)]
        if step == "mT":
            yield "mT", a, g


def loop1_fills():
    names = [("xT", c) for c in range(CT)]
    names += [(w, t) for t in range(TT) for w in ("q", "k", "v")]
    names += attention_fills(0)
    names += [("wo", t) for t in range(TT)]
    names += [("xrT", c) for c in range(CT)]
    names += [("lat", m) for m in range(2)]
    names += [(w, t) for t in range(TT) for w in ("q2", "k2", "v2")]
    names += attention_fills(1)
    names += [("wo2", t) for t in range(TT)]
    return names


def loop2_fills():
    names = [("xT", c) for c in range(CT)] + [("z", 0), ("zT", 0)]
    for step in expert_order():
        if step[0] == "GU":
            names += [("gate", *step[1:]), ("up", *step[1:])]
        else:
            names += [("down", step[1], t) for t in range(TT)]
    return names


def expert_order():
    for e in range(NE):
        yield "GU", e, 0
        if e:
            yield "D", e - 1
        yield "GU", e, 1
    yield "D", NE - 1


def attention_layers(nc, x, weights, tables, ln1_w, x1_out, h_out, blocks):
    w_qkv, w_o, kv_d, q_d, k_u, v_u, q_u, rope_k, rope_q, o_w = weights
    rope1_d, rope2_d = tables
    with ExitStack() as ctx:
        def sb(name, shape, dt=F32):
            return ctx.enter_context(nc.sbuf_tensor(name, shape, dt))

        signals = []

        def signal(name, per_pass):
            signals.append(Signal(ctx.enter_context(nc.semaphore(name)), per_pass))
            return signals[-1]

        wqkv = sb("wqkv", [P, CT, 3 * D])
        wo = sb("wo", [P, 2, CT, D])
        wlat = sb("wlat", [P, CT, 2, LAT])
        wku = sb("wku", [P, NH * RD])
        wvu = sb("wvu", [P, D])
        wq2 = sb("wq2", [P, NH, 2, RD])
        wkr = sb("wkr", [P, CT, NH * RD])
        rope1 = sb("rope1", [P, TT, 2, HD])
        rope2 = sb("rope2", [P, TT, 2, RD])
        ln1w = sb("ln1w", [P, CT])
        ident = sb("ident", [P, P])
        ones = sb("ones", [P, HD])
        mask = sb("mask", [P, T])

        x_in = sb("x_in", [P, TT, D])
        x1 = sb("x1", [P, TT, D])
        xin = sb("xin", [P, TT, D])
        xT = sb("xT", [P, CT, T])
        q = sb("q", [P, TT, D])
        k = sb("k", [P, TT, D])
        v = sb("v", [P, TT, D])
        latT = sb("latT", [P, 2, T])
        turned = sb("turned", [P, 2, 2, D])
        high = sb("high", [P, 2, T], F32R)
        low = sb("low", [P, 2, T], F32R)
        qs = [sb(f"qs{n}", [P, GH, T], F32R) for n in range(STACKS)]
        ks = [sb(f"ks{n}", [P, GH, T], F32R) for n in range(STACKS)]
        probs = sb("probs", [P, 2, GH, T])
        total = sb("total", [P, T])
        unused = sb("unused", [P, TT, T], BF16)
        rowmax = sb("rowmax", [P, 2, GH * TT])
        negmax = sb("negmax", [GH * TT, 2, P], F32R)
        stats = sb("stats", [P, TT, 6])
        meanvar = sb("meanvar", [P, TT, 2])
        rstd = sb("rstd", [P, TT])
        padded = sb("padded", [P, TT])
        minus_half = sb("minus_half", [P, TT])
        rms = sb("rms", [P, TT])
        rms2 = sb("rms2", [P, TT])
        both = sb("both", [P, TT])

        ring = ctx.enter_context(nc.psum_tensor("ring", [P, 2, 512], F32))
        scoresT = ctx.enter_context(nc.psum_tensor("scoresT", [P, 2, 2, 512], F32))
        out_ps = ctx.enter_context(nc.psum_tensor("out_ps", [P, 512], F32))
        sum_ps = ctx.enter_context(nc.psum_tensor("sum_ps", [P, 512], F32))

        names = loop1_fills()
        if len(names) % 2:
            raise AssertionError("an odd number of fills")
        filled = ctx.enter_context(nc.semaphore("ring_filled"))
        freed = [ctx.enter_context(nc.semaphore(f"ring_freed{n}")) for n in range(2)]
        banks = Banks(ring, filled, freed, names)

        weights_in = ctx.enter_context(nc.semaphore("weights_in"))
        consts = ctx.enter_context(nc.semaphore("consts"))
        consts_step = ctx.enter_context(nc.semaphore("consts_step"))
        N_CONSTS = 4 + STACKS
        x_loaded = signal("x_loaded", 16)
        stats_done = signal("stats_done", 3 * TT)
        meanvar_done = signal("meanvar_done", 3 * TT)
        padded_done = signal("padded_done", 3)
        rstd_done = signal("rstd_done", 3)
        rms_step = signal("rms_step", 5)
        normed = signal("normed", TT)
        y_normed = signal("y_normed", TT)
        x1_done = signal("x1_done", TT)
        xin_done = signal("xin_done", TT)
        xr_done = signal("xr_done", TT)
        x1_stored = signal("x1_stored", 16)
        h_stored = signal("h_stored", 16)
        cos_done = signal("cos_done", 4 * TT)
        rotated = signal("rotated", 4 * TT)
        plain_done = signal("plain_done", 2 * TT)
        high_done = signal("high_done", 2 * 2 * NG)
        PER_STACK = 6 * GH
        stacked = signal("stacked", 2 * NG * PER_STACK * 16)
        max_done = signal("max_done", 2 * NH)
        negmax_in = signal("negmax_in", 2 * NG * 16)
        st_filled = signal("st_filled", 2 * NG * TT * 2)
        exp_done = signal("exp_done", 2 * NG * TT * 2)
        pool_turn = ctx.enter_context(nc.semaphore("pool_turn"))
        dve_turn = ctx.enter_context(nc.semaphore("dve_turn"))
        sp_turn = ctx.enter_context(nc.semaphore("sp_turn"))
        causal = signal("causal", 2 * NG * TT)
        pv_done = signal("pv_done", 2 * NG * TT)
        total_done = signal("total_done", 2 * NG)
        out_done = signal("out_done", 2 * NG)

        with nc.Block() as block:
            @block.sync
            def _(sp):
                for s in signals:
                    sp.sem_inc(s.sem, 1)
                for sem in [filled, *freed]:
                    sp.sem_inc(sem, 1)

        with nc.Block() as block:

            @block.sync
            def _(sp):
                loads = [
                    (rope1[:, :, :, :], rope1_d), (rope2[:, :, :, :], rope2_d),
                    (ln1w[:, :], ln1_w),
                    (wqkv[:, :, :], w_qkv.rearrange("(c p) n -> p c n", p=P)),
                    (wo[:, 0], w_o.rearrange("(c p) n -> p c n", p=P)),
                    (wlat[:, :, 0, :], kv_d.rearrange("(c p) n -> p c n", p=P)),
                    (wlat[:, :, 1, :], q_d.rearrange("(c p) n -> p c n", p=P)),
                    (wku[:, :], k_u), (wvu[:, :], v_u),
                    (wq2[:, :, 0, :], q_u.rearrange("p (h d) -> p h d", h=NH)),
                    (wq2[:, :, 1, :], rope_q.rearrange("p (h d) -> p h d", h=NH)),
                    (wkr[:, :, :], rope_k.rearrange("(c p) n -> p c n", p=P)),
                    (wo[:, 1], o_w.rearrange("(c p) n -> p c n", p=P)),
                ]
                assert len(loads) == N_LOADS
                for to, of in loads:
                    sp.dma_start(to, of).then_inc(weights_in, 16)
                sp.wait_ge(consts, N_CONSTS)

                def stack(i, n):
                    a, g = divmod(n, NG)
                    to_q, to_k = qs[n % STACKS], ks[n % STACKS]
                    sp.wait_ge(*high_done.after(i, 2 * (n + 1)))
                    sp.sem_inc(sp_turn, 1)
                    sp.wait_ge(*banks.out(i, ("qT", a, g)))
                    sp.sem_inc(sp_turn, 1)
                    sp.wait_ge(*banks.out(i, ("kT", a, g)))
                    sp.sem_inc(sp_turn, 1)
                    sp.wait_ge(*st_filled.after(i, max(0, 2 * TT * (n - STACKS + 1))))
                    sp.sem_inc(sp_turn, 1)
                    for which, to, slots in ((0, to_q, (high, low, high)), (1, to_k, (high, high, low))):
                        for s, part in enumerate(slots):
                            for h in range(GH):
                                sp.dma_start(to[s * HD:(s + 1) * HD, h, :].bitcast(F32),
                                             part[h * HD:(h + 1) * HD, which, :].bitcast(F32)).then_inc(stacked.sem, 16)

                def put_negmax(i, n):
                    a, g = divmod(n, NG)
                    sp.wait_ge(*banks.out(i, ("mT", a, g)))
                    sp.sem_inc(sp_turn, 1)
                    sp.dma_start(qs[n % STACKS][ROWMAX:ROWMAX + 1, :, :].rearrange("o h t -> o (h t)").bitcast(F32),
                                 negmax[:, n % 2, :].bitcast(F32)).then_inc(negmax_in.sem, 16)

                with sp.Fori(0, blocks) as i:
                    sp.wait_ge(*x1_done.after(i, 0))
                    sp.sem_inc(sp_turn, 1)
                    sp.dma_start(x_in[:, :, :], x[bass.ds(i, 1), :, :]
                                 .rearrange("o (t p) c -> p (o t) c", p=P)).then_inc(x_loaded.sem, 16)
                    for a in range(2):
                        for step, g, _ in attention_order(a):
                            if step == "qkT":
                                stack(i, a * NG + g)
                            if step == "mT":
                                put_negmax(i, a * NG + g)
                        if a == 0:
                            sp.wait_ge(*x1_done.after(i, TT))
                            sp.sem_inc(sp_turn, 1)
                            sp.dma_start(x1_out[bass.ds(i, 1), :, :]
                                         .rearrange("o (t p) c -> p (o t) c", p=P), x1[:, :, :])\
                              .then_inc(x1_stored.sem, 16)
                    for t in range(TT - 2, TT):
                        sp.wait_ge(*banks.out(i, ("wo2", t)))
                        sp.sem_inc(sp_turn, 1)
                    sp.dma_start(h_out[bass.ds(i, 1), :, :]
                                 .rearrange("o (t p) c -> p (o t) c", p=P), k[:, :, :])\
                      .then_inc(h_stored.sem, 16)
                sp.wait_ge(*x1_stored.after(blocks - 1, 16))
                sp.wait_ge(*h_stored.after(blocks - 1, 16))

            @block.gpsimd
            def _(pool):
                pool.memset(ones[:, :], 1.0).then_inc(consts, 1)
                pool.memset(minus_half[:, :], -0.5).then_inc(consts, 1)
                pool.memset(ident[:, :], 0.0).then_inc(consts_step, 1)
                pool.memset(mask[:, :], 0.0).then_inc(consts_step, 1)
                pool.wait_ge(consts_step, 2)
                pool.affine_select(out=ident[:, :], in_=ident[:, :], compare_op=ALU.not_equal, fill=1.0,
                                   base=0, pattern=[[-1, P]], channel_multiplier=1).then_inc(consts, 1)
                pool.affine_select(out=mask[:, :], in_=mask[:, :], compare_op=ALU.is_ge, fill=MASKED,
                                   base=T - P, pattern=[[-1, T]], channel_multiplier=1).then_inc(consts, 1)

                def take_rstd(i, n):
                    pool.wait_ge(*meanvar_done.after(i, TT * (n + 1)))
                    pool.sem_inc(pool_turn, 1)
                    pool.tensor_scalar(padded[:, :], meanvar[:, :, 1], EPS, None, ALU.add).then_inc(padded_done.sem, 1)
                    pool.wait_ge(*padded_done.after(i, n + 1))
                    pool.tensor_tensor(rstd[:, :], padded[:, :], minus_half[:, :], ALU.pow)\
                        .then_inc(rstd_done.sem, 1)

                def add_rotated(i, r, to):
                    n, t = divmod(r, TT) if r < 2 * TT else (0, 0)
                    pool.wait_ge(*cos_done.after(i, r + 1))
                    pool.wait_ge(*banks.out(i, rotation_fill(r)))
                    w = to.shape[-1]
                    a = turned[:, r % 2, 0, 0:NH * w].rearrange("p (h d) -> p h d", h=NH)
                    b = turned[:, r % 2, 1, 0:NH * w].rearrange("p (h d) -> p h d", h=NH)
                    pool.tensor_tensor(to, a, b, ALU.add).then_inc(rotated.sem, 1)

                def cut(i, n):
                    pool.wait_ge(*exp_done.after(i, 2 * (n + 1)))
                    pool.sem_inc(pool_turn, 1)
                    diagonal = probs[:, n % 2, :, 0:P]
                    pool.affine_select(out=diagonal, in_=diagonal, compare_op=ALU.is_ge, fill=0.0,
                                       base=0, pattern=[[0, GH], [1, P]], channel_multiplier=-1)\
                        .then_inc(causal.sem, 1)

                pool.wait_ge(consts, N_CONSTS)
                with pool.Fori(0, blocks) as i:
                    take_rstd(i, 0)
                    pool.wait_ge(*h_stored.after(i, 0))
                    for r in range(2 * TT):
                        t, which = divmod(r, 2)
                        add_rotated(i, r, (q, k)[which][:, t, :].rearrange("p (h d) -> p h d", h=NH))
                    for n in range(NG * TT):
                        cut(i, n)
                    take_rstd(i, 1)
                    take_rstd(i, 2)
                    pool.wait_ge(*rstd_done.after(i, 3))
                    pool.sem_inc(pool_turn, 1)
                    pool.tensor_tensor(rms[:, :], rstd[:, :], rstd[:, :], ALU.mult).then_inc(rms_step.sem, 1)
                    pool.wait_ge(*rms_step.after(i, 1))
                    pool.tensor_tensor(rms2[:, :], rms[:, :], meanvar[:, :, 1], ALU.mult).then_inc(rms_step.sem, 1)
                    pool.wait_ge(*rms_step.after(i, 2))
                    pool.sem_inc(pool_turn, 1)
                    pool.tensor_scalar(padded[:, :], rms2[:, :], EPS, None, ALU.add).then_inc(rms_step.sem, 1)
                    pool.wait_ge(*rms_step.after(i, 3))
                    pool.tensor_tensor(rms[:, :], padded[:, :], minus_half[:, :], ALU.pow).then_inc(rms_step.sem, 1)
                    pool.wait_ge(*rms_step.after(i, 4))
                    pool.tensor_tensor(both[:, :], rms[:, :], rstd[:, :], ALU.mult).then_inc(rms_step.sem, 1)
                    for r in range(2 * TT, 4 * TT):
                        t, which = divmod(r - 2 * TT, 2)
                        rows = (q, k)[which][:, t, :].rearrange("p (h s d) -> p h s d", h=NH, s=2)
                        add_rotated(i, r, rows[:, :, 1, :])
                    for n in range(NG * TT, 2 * NG * TT):
                        cut(i, n)

            @block.scalar
            def _(act):
                act.wait_ge(weights_in, 16 * N_LOADS)

                def copy(i, name, to, scale=1.0):
                    act.wait_ge(*banks.full(i, name))
                    act.activation(to, banks.bank(name), ACT.Copy, scale=scale)\
                       .then_inc(banks.release(name), 1)

                def take_high(i, n):
                    a, g = divmod(n, NG)
                    act.wait_ge(*stacked.after(i, 16 * PER_STACK * n))
                    for which, name in enumerate(("qT", "kT")):
                        act.wait_ge(*banks.full(i, (name, a, g)))
                        act.activation(high[:, which, :], banks.bank((name, a, g)), ACT.Copy)\
                           .then_inc(high_done.sem, 1)

                def take_negmax(i, n):
                    a, g = divmod(n, NG)
                    act.wait_ge(*negmax_in.after(i, 16 * max(0, n - 1)))
                    act.wait_ge(*banks.full(i, ("mT", a, g)))
                    act.activation(negmax[:, n % 2, :], banks.bank(("mT", a, g))[0:GH * TT, 0:P], ACT.Copy,
                                   scale=-1.0).then_inc(banks.release(("mT", a, g)), 1)

                def exps(i, n, j):
                    m = n * TT + j
                    act.wait_ge(*pv_done.after(i, max(0, m - 1)))
                    first, width = (P, P) if j == TT - 1 else (0, T - P * j)
                    for pair in range(2):
                        u = 2 * m + pair
                        act.wait_ge(*st_filled.after(i, u + 1))
                        act.activation(probs[:, m % 2, 2 * pair:2 * pair + 2, 0:width],
                                       scoresT[:, u % 2, :, first:first + width], ACT.Exp, scale=SCALE)\
                           .then_inc(exp_done.sem, 1)

                def attend(i, a):
                    for step, g, j in attention_order(a):
                        if step == "qkT":
                            take_high(i, a * NG + g)
                        if step == "mT":
                            take_negmax(i, a * NG + g)
                        if step == "ST":
                            exps(i, a * NG + g, j)

                with act.Fori(0, blocks) as i:
                    for c in range(CT):
                        copy(i, ("xT", c), xT[:, c, :])
                    for t in range(TT):
                        copy(i, ("v", t), v[:, t, :])
                    attend(i, 0)
                    for t in range(TT):
                        copy(i, ("wo", t), k[:, t, :])
                    for c in range(CT):
                        copy(i, ("xrT", c), xT[:, c, :], scale=ln1w[:, c:c + 1])
                    for m in range(2):
                        copy(i, ("lat", m), latT[:, m, :])
                    for t in range(TT):
                        copy(i, ("v2", t), v[:, t, :])
                    attend(i, 1)

            @block.vector
            def _(dve):
                for n in range(STACKS):
                    dve.memset(ks[n][ROWMAX:ROWMAX + 1, :, :].bitcast(F32), 1.0).then_inc(consts, 1)
                dve.wait_ge(consts, N_CONSTS)
                dve.wait_ge(weights_in, 16 * N_LOADS)

                def take_stats(i, n, rows):
                    for t in range(TT):
                        if n == 0:
                            dve.wait_ge(*x_loaded.after(i, 16))
                        if n == 1:
                            dve.wait_ge(*banks.out(i, ("wo", t)))
                        if n == 2:
                            dve.wait_ge(*x1_done.after(i, t + 1))
                        dve.bn_stats(stats[:, t, :], rows[:, t, :]).then_inc(stats_done.sem, 1)
                    for t in range(TT):
                        dve.wait_ge(*stats_done.after(i, TT * n + t + 1))
                        dve.sem_inc(dve_turn, 1)
                        dve.bn_aggr(meanvar[:, t, :], stats[:, t, :]).then_inc(meanvar_done.sem, 1)

                def norm(to, rows, t, scale, done):
                    dve.tensor_scalar(to[:, t, :], rows[:, t, :], meanvar[:, t, 0:1], scale[:, t:t + 1],
                                      ALU.subtract, ALU.mult).then_inc(done.sem, 1)

                def rotate(i, r, rows, table):
                    name = rotation_fill(r)
                    half = table.shape[-1] // 2
                    dve.wait_ge(*rotated.after(i, max(0, r - 1)))
                    shape = [P, NH, 2, half]
                    a, b = (turned[:, r % 2, s, 0:NH * 2 * half]
                            .rearrange("p (h s d) -> p h s d", h=NH, s=2) for s in range(2))
                    cos, sin = (table[:, s, :].rearrange("p (s d) -> p s d", s=2).unsqueeze(1)
                                .to_broadcast(shape) for s in range(2))
                    dve.tensor_tensor(a, rows, cos, ALU.mult).then_inc(cos_done.sem, 1)
                    dve.tensor_tensor(b, rows[:, :, ::-1, :], sin, ALU.mult).then_inc(banks.release(name), 1)

                def take_low(i, n):
                    a, g = divmod(n, NG)
                    for which, name in enumerate(("qT", "kT")):
                        dve.wait_ge(*high_done.after(i, 2 * n + which + 1))
                        dve.tensor_tensor(low[:, which, :], banks.bank((name, a, g)), high[:, which, :],
                                          ALU.subtract).then_inc(banks.release((name, a, g)), 1)

                def maxima(i, n, h):
                    a, g = divmod(n, NG)
                    before = divmod(GH * n + h - 1, GH)
                    for t in range(TT):
                        name = ("S", a, g, h, max(0, t - 1))
                        first = P * 2 * (t == 1)
                        dve.wait_ge(*banks.full(i, name))
                        if t == 0 or before[0] < 0:
                            dve.wait_ge(*max_done.after(i, GH * n + h))
                        else:
                            dve.wait_ge(*banks.out(i, ("S", *divmod(before[0], NG), before[1], t - 1)))
                        dve.sem_inc(dve_turn, 1)
                        width = P * (t + 1)
                        ins = dve.tensor_tensor_reduce(
                            unused[:, t, 0:width], banks.bank(name)[:, first:first + width],
                            mask[:, T - width:T], 1.0, MASKED, ALU.add, ALU.max,
                            rowmax[:, n % 2, TT * h + t:TT * h + t + 1])
                        if t == 0:
                            ins.then_inc(max_done.sem, 1)
                        else:
                            ins.then_inc(banks.release(name), 1)

                def close(i, n):
                    dve.wait_ge(*pv_done.after(i, TT * (n + 1)))
                    dve.reciprocal(total[:, :], sum_ps[:, :]).then_inc(total_done.sem, 1)
                    dve.wait_ge(*total_done.after(i, n + 1))
                    dve.tensor_tensor(xT[:, n % NG, :], out_ps[:, :], total[:, :], ALU.mult)\
                       .then_inc(out_done.sem, 1)

                def attend(i, a):
                    for step, g, h in attention_order(a):
                        n = a * NG + g
                        if step == "qkT":
                            take_low(i, n)
                        if step == "S":
                            if h == 0 and g >= 2:
                                dve.wait_ge(*banks.full(i, ("mT", a, g - 2)))
                            maxima(i, n, h)
                        if step == "PV" and h == TT - 1:
                            close(i, n)

                with dve.Fori(0, blocks) as i:
                    take_stats(i, 0, x_in)
                    dve.wait_ge(*rstd_done.after(i, 1))
                    dve.wait_ge(*x1_stored.after(i, 0))
                    for t in range(TT):
                        norm(x1, x_in, t, rstd, normed)
                    for r in range(2 * TT):
                        t, which = divmod(r, 2)
                        dve.wait_ge(*banks.full(i, rotation_fill(r)))
                        rows = banks.bank(rotation_fill(r)).rearrange("p (h s d) -> p h s d", h=NH, s=2)
                        rotate(i, r, rows, rope1[:, t])
                    attend(i, 0)
                    take_stats(i, 1, k)
                    dve.wait_ge(*rstd_done.after(i, 2))
                    for t in range(TT):
                        norm(q, k, t, rstd, y_normed)
                    for t in range(TT):
                        dve.wait_ge(*y_normed.after(i, t + 1))
                        dve.tensor_tensor(x1[:, t, :], q[:, t, :], x_in[:, t, :], ALU.add).then_inc(x1_done.sem, 1)
                    take_stats(i, 2, x1)
                    dve.wait_ge(*rstd_done.after(i, 3))
                    for t in range(TT):
                        norm(xin, x1, t, rstd, xin_done)
                    dve.wait_ge(*rms_step.after(i, 5))
                    for t in range(TT):
                        norm(q, x1, t, both, xr_done)
                    for r in range(2 * TT, 4 * TT):
                        t, which = divmod(r - 2 * TT, 2)
                        name = rotation_fill(r)
                        dve.wait_ge(*banks.full(i, name))
                        to = (q, k)[which][:, t, :].rearrange("p (h s d) -> p h s d", h=NH, s=2)[:, :, 0, :]
                        if which == 0:
                            both_parts = banks.bank(name).rearrange("p (h s d) -> p s h d", h=NH, s=2)
                        else:
                            both_parts = banks.bank(name).rearrange("p (s h d) -> p s h d", h=NH, s=2)
                        dve.tensor_copy(to, both_parts[:, 0]).then_inc(plain_done.sem, 1)
                        rows = both_parts[:, 1].rearrange("p h (s d) -> p h s d", s=2)
                        rotate(i, r, rows, rope2[:, t])
                    attend(i, 1)
                    for t in range(TT):
                        dve.wait_ge(*banks.full(i, ("wo2", t)))
                        dve.tensor_tensor(k[:, t, :], banks.bank(("wo2", t)), xin[:, t, :], ALU.add)\
                           .then_inc(banks.release(("wo2", t)), 1)

            @block.tensor
            def _(pe):
                pe.wait_ge(consts, N_CONSTS)
                pe.wait_ge(weights_in, 16 * N_LOADS)
                def transpose_tiles(i, name, rows, c):
                    to = banks.bank(name)
                    pe.wait_ge(*banks.empty(i, name))
                    for t in range(TT):
                        ins = pe.transpose(to[:, t * P:(t + 1) * P], rows[:, t, c * P:(c + 1) * P], ident[:, :])
                    ins.then_inc(filled, 1)

                def scores(i, n, h):
                    a, g = divmod(n, NG)
                    to_q, to_k = qs[n % STACKS], ks[n % STACKS]
                    if h == 0:
                        pe.wait_ge(*stacked.after(i, 16 * PER_STACK * (n + 1)))
                    for part, tiles in enumerate(((0, 1), (2,), (3,))):
                        name = ("S", a, g, h, part)
                        to = banks.bank(name)
                        pe.wait_ge(*banks.empty(i, name))
                        for t in tiles:
                            width = max(2 * P, P * (t + 1))
                            first = 2 * P * (t == 1)
                            ins = pe.matmul(to[:, first:first + width],
                                            to_q[0:ROWMAX, h, t * P:(t + 1) * P],
                                            to_k[0:ROWMAX, h, 0:width], start=True, stop=True)
                        ins.then_inc(filled, 1)

                def transpose_max(i, n):
                    a, g = divmod(n, NG)
                    name = ("mT", a, g)
                    to = banks.bank(name)
                    pe.wait_ge(*banks.empty(i, name))
                    pe.wait_ge(*max_done.after(i, GH * (n + 1)))
                    pe.wait_ge(*banks.out(i, ("S", a, g, GH - 1, 2)))
                    pe.transpose(to[0:GH * TT, 0:P], rowmax[:, n % 2, :], ident[:, :]).then_inc(filled, 1)

                def scores_less_max(i, n, j):
                    if j == 0:
                        pe.wait_ge(*negmax_in.after(i, 16 * (n + 1)))
                    first = min(P * j, T - 2 * P)
                    for pair in range(2):
                        u = 2 * (TT * n + j) + pair
                        pe.wait_ge(*exp_done.after(i, max(0, u - 1)))
                        for s in range(2):
                            h = 2 * pair + s
                            ins = pe.matmul(scoresT[:, u % 2, s, 0:T - first],
                                            ks[n % STACKS][0:ROWMAX + 1, h, j * P:(j + 1) * P],
                                            qs[n % STACKS][0:ROWMAX + 1, h, first:T], start=True, stop=True)
                        ins.then_inc(st_filled.sem, 1)

                def times_v(i, n, j):
                    g = n % NG
                    m = TT * n + j
                    if j == 0:
                        pe.wait_ge(*out_done.after(i, n))
                    pe.wait_ge(*causal.after(i, m + 1))
                    for to, is_sum in ((out_ps, False), (sum_ps, True)):
                        for h in range(GH):
                            head = (GH * g + h) * HD
                            left = ones[:, :] if is_sum else v[:, j, head:head + HD]
                            ins = pe.matmul(to[h * HD:(h + 1) * HD, P * j:T], left,
                                            probs[:, m % 2, h, 0:T - P * j],
                                            start=(j == 0), stop=(j == TT - 1))
                    ins.then_inc(pv_done.sem, 1)

                def attend(i, a):
                    for step, g, h in attention_order(a):
                        n = a * NG + g
                        if step == "qkT":
                            transpose_tiles(i, ("qT", a, g), q, g)
                            transpose_tiles(i, ("kT", a, g), k, g)
                        if step == "S":
                            scores(i, n, h)
                        if step == "mT":
                            transpose_max(i, n)
                        if step == "ST":
                            scores_less_max(i, n, h)
                        if step == "PV":
                            times_v(i, n, h)

                def product(to, pairs):
                    for n, (left, right) in enumerate(pairs):
                        ins = pe.matmul(to, left, right, start=(n == 0), stop=(n == len(pairs) - 1))
                    return ins

                def tile_of(rows_T, c, t):
                    return rows_T[:, c, t * P:(t + 1) * P]

                with pe.Fori(0, blocks) as i:
                    pe.wait_ge(*normed.after(i, TT))
                    for c in range(CT):
                        transpose_tiles(i, ("xT", c), x1, c)
                    pe.wait_ge(*banks.out(i, ("xT", CT - 1)))
                    for t in range(TT):
                        for n, name in enumerate(("q", "k", "v")):
                            to = banks.bank((name, t))
                            pe.wait_ge(*banks.empty(i, (name, t)))
                            product(to, [(tile_of(xT, c, t), wqkv[:, c, n * D:(n + 1) * D])
                                         for c in range(CT)]).then_inc(filled, 1)
                    pe.wait_ge(*rotated.after(i, 2 * TT))
                    pe.wait_ge(*banks.out(i, ("v", TT - 1)))
                    attend(i, 0)
                    pe.wait_ge(*out_done.after(i, NG))
                    for t in range(TT):
                        to = banks.bank(("wo", t))
                        pe.wait_ge(*banks.empty(i, ("wo", t)))
                        product(to, [(tile_of(xT, c, t), wo[:, 0, c, :]) for c in range(CT)]).then_inc(filled, 1)
                    pe.wait_ge(*xr_done.after(i, TT))
                    for c in range(CT):
                        transpose_tiles(i, ("xrT", c), q, c)
                    pe.wait_ge(*banks.out(i, ("xrT", CT - 1)))
                    for m in range(2):
                        to = banks.bank(("lat", m))
                        pe.wait_ge(*banks.empty(i, ("lat", m)))
                        product(to, [(wlat[:, c, m, :], xT[:, c, :]) for c in range(CT)]).then_inc(filled, 1)
                    pe.wait_ge(*banks.out(i, ("lat", 1)))
                    for t in range(TT):
                        kv, qd = tile_of(latT, 0, t), tile_of(latT, 1, t)
                        to = banks.bank(("q2", t))
                        pe.wait_ge(*banks.empty(i, ("q2", t)))
                        product(to, [(qd, wq2[:, :, :, :].rearrange("p h s d -> p (h s d)"))]).then_inc(filled, 1)
                        to = banks.bank(("k2", t))
                        pe.wait_ge(*banks.empty(i, ("k2", t)))
                        product(to[:, 0:NH * RD], [(kv, wku[:, :])])
                        product(to[:, NH * RD:D], [(tile_of(xT, c, t), wkr[:, c, :]) for c in range(CT)])\
                            .then_inc(filled, 1)
                        to = banks.bank(("v2", t))
                        pe.wait_ge(*banks.empty(i, ("v2", t)))
                        product(to, [(kv, wvu[:, :])]).then_inc(filled, 1)
                    pe.wait_ge(*plain_done.after(i, 2 * TT))
                    pe.wait_ge(*rotated.after(i, 4 * TT))
                    pe.wait_ge(*banks.out(i, ("v2", TT - 1)))
                    attend(i, 1)
                    pe.wait_ge(*out_done.after(i, 2 * NG))
                    for t in range(TT):
                        to = banks.bank(("wo2", t))
                        pe.wait_ge(*banks.empty(i, ("wo2", t)))
                        product(to, [(tile_of(xT, c, t), wo[:, 1, c, :]) for c in range(CT)]).then_inc(filled, 1)


N_LOADS = 13


def rotation_fill(r):
    t, which = divmod(r % (2 * TT), 2)
    return (("q", "k"), ("q2", "k2"))[r // (2 * TT)][which], t


def expert_layer(nc, h_in, x1_in, ln2_w, weights, out, blocks):
    sh_gate, sh_up, sh_down, r_gate, r_up, r_down, router_w, router_b = weights
    with ExitStack() as ctx:
        def sb(name, shape, dt=F32):
            return ctx.enter_context(nc.sbuf_tensor(name, shape, dt))

        signals = []

        def signal(name, per_pass):
            signals.append(Signal(ctx.enter_context(nc.semaphore(name)), per_pass))
            return signals[-1]

        wg = sb("wg", [P, NE, CT, FF])
        wu = sb("wu", [P, NE, CT, FF])
        wd = sb("wd", [P, NE, FT, D])
        wr = sb("wr", [P, CT, NR])
        rb = sb("rb", [NR, 1])
        ln2w = sb("ln2w", [P, CT])
        ident = sb("ident2", [P, P])
        number = sb("number", [P, NR])
        h = sb("h", [P, 2, TT, D])
        x1 = sb("x1b", [P, 2, TT, D])
        xr = sb("xr", [P, TT, D])
        xT = sb("xT2", [P, CT, T])
        actT = sb("actT", [P, 2, FT, T])
        tanh = sb("tanh", [P, 2, T])
        gated = sb("gated", [P, 2, T])
        zT = sb("zT", [P, T])
        half = sb("half", [P, TT, NR])
        chance = sb("chance", [P, TT, 8])
        best = sb("best", [P, TT, 8])
        where = sb("where", [P, TT, 8], U32)
        wheref = sb("wheref", [P, TT, 2])
        den = sb("den", [P, TT])
        rden = sb("rden", [P, TT])
        share = sb("share", [P, TT, 2])
        part = sb("part", [P, 2, TT, NR])
        gain = sb("gain", [P, TT, NR])
        unused = sb("unused2", [P, TT, D])
        square = sb("square", [P, TT])
        padded = sb("padded2", [P, 2, TT])
        minus_half = sb("minus_half2", [P, TT])
        rms = sb("rms_h", [P, TT])
        stats = sb("stats2", [P, TT, 6])
        meanvar = sb("meanvar2", [P, TT, 2])
        rstd = sb("rstd2", [P, TT])

        names = loop2_fills()
        ring = ctx.enter_context(nc.psum_tensor("ring2", [P, 7, 512], F32))
        filled = ctx.enter_context(nc.semaphore("ring2_filled"))
        freed = [ctx.enter_context(nc.semaphore(f"ring2_freed{n}")) for n in range(7)]
        banks = Banks(ring, filled, freed, names)

        small_in = ctx.enter_context(nc.semaphore("small_in"))
        expert_in = [ctx.enter_context(nc.semaphore(f"expert_in{e}")) for e in range(NE)]
        consts = ctx.enter_context(nc.semaphore("consts2"))
        consts_step = ctx.enter_context(nc.semaphore("consts2_step"))
        N_CONSTS = 5
        padded_done = signal("padded2_done", 2)
        N_SMALL = 3
        h_loaded = signal("h_loaded", 16)
        x1_loaded = signal("x1_loaded", 16)
        squared = signal("squared", TT)
        rms_done = signal("rms_done", 1)
        xr_done = signal("xr_done2", TT)
        pool_turn = ctx.enter_context(nc.semaphore("pool_turn2"))
        dve_turn = ctx.enter_context(nc.semaphore("dve_turn2"))
        sp_turn = ctx.enter_context(nc.semaphore("sp_turn2"))
        chance_done = signal("chance_done", 1)
        ROUTE = 2 * TT + 4 + 2 * TT + 1
        route_step = signal("route_step", ROUTE)
        tanh_done = signal("tanh_done", NE * FT)
        gated_step = signal("gated_step", 0)
        stats_done = signal("stats2_done", TT)
        meanvar_done = signal("meanvar2_done", TT)
        rstd_done = signal("rstd2_done", 1)
        closed = signal("closed", TT)
        out_ready = signal("out_ready", TT)
        stored = signal("stored", 16)

        with nc.Block() as block:
            @block.sync
            def _(sp):
                for s in signals:
                    sp.sem_inc(s.sem, 1)
                for sem in [filled, *freed]:
                    sp.sem_inc(sem, 1)

        with nc.Block() as block:
            @block.sync
            def _(sp):
                sp.dma_start(ln2w[:, :], ln2_w).then_inc(small_in, 16)
                sp.dma_start(wr[:, :, :], router_w.rearrange("(c p) n -> p c n", p=P)).then_inc(small_in, 16)
                sp.dma_start(rb[:, :], router_b).then_inc(small_in, 16)
                with sp.Fori(0, blocks) as i:
                    sp.wait_ge(*stored.after(i, 0))
                    sp.sem_inc(sp_turn, 1)
                    rows = "o (t p) c -> p (o t) c"
                    sp.dma_start(h[:, 0], h_in[bass.ds(i, 1), :, :].rearrange(rows, p=P)).then_inc(h_loaded.sem, 16)
                    sp.dma_start(x1[:, 0], x1_in[bass.ds(i, 1), :, :].rearrange(rows, p=P)).then_inc(x1_loaded.sem, 16)
                    sp.wait_ge(*out_ready.after(i, TT))
                    sp.sem_inc(sp_turn, 1)
                    sp.dma_start(out[bass.ds(i, 1), :, :].rearrange(rows, p=P), x1[:, 0]).then_inc(stored.sem, 16)
                sp.wait_ge(*stored.after(blocks - 1, 16))

            @block.gpsimd
            def _(pool):
                pool.memset(ident[:, :], 0.0).then_inc(consts_step, 1)
                pool.memset(zT[:, :], 0.0).then_inc(consts, 1)
                pool.memset(minus_half[:, :], -0.5).then_inc(consts, 1)
                pool.memset(chance[:, :, :], -1.0).then_inc(consts, 1)
                pool.iota(number[:, :], pattern=[[1, NR]], base=0, channel_multiplier=0,
                          allow_small_or_imprecise_dtypes=True).then_inc(consts, 1)
                pool.wait_ge(consts_step, 1)
                pool.affine_select(out=ident[:, :], in_=ident[:, :], compare_op=ALU.not_equal, fill=1.0,
                                   base=0, pattern=[[-1, P]], channel_multiplier=1).then_inc(consts, 1)
                with pool.Fori(0, blocks) as i:
                    pool.wait_ge(*squared.after(i, TT))
                    pool.sem_inc(pool_turn, 1)
                    pool.tensor_scalar(padded[:, 0, :], square[:, :], EPS, None, ALU.add).then_inc(padded_done.sem, 1)
                    pool.wait_ge(*padded_done.after(i, 1))
                    pool.tensor_tensor(rms[:, :], padded[:, 0, :], minus_half[:, :], ALU.pow)\
                        .then_inc(rms_done.sem, 1)
                    pool.wait_ge(*meanvar_done.after(i, TT))
                    pool.sem_inc(pool_turn, 1)
                    pool.tensor_scalar(padded[:, 1, :], meanvar[:, :, 1], EPS, None, ALU.add).then_inc(padded_done.sem, 1)
                    pool.wait_ge(*padded_done.after(i, 2))
                    pool.tensor_tensor(rstd[:, :], padded[:, 1, :], minus_half[:, :], ALU.pow)\
                        .then_inc(rstd_done.sem, 1)

            @block.scalar
            def _(act):
                for e in range(NE):
                    gate, up, down = (sh_gate, sh_up, sh_down) if e == 0 else (r_gate[e - 1], r_up[e - 1], r_down[e - 1])
                    for to, of in ((wg, gate), (wu, up), (wd, down)):
                        act.dma_start(to[:, e], of.rearrange("(c p) n -> p c n", p=P)).then_inc(expert_in[e], 16)
                act.wait_ge(consts, N_CONSTS)
                act.wait_ge(small_in, 16 * N_SMALL)
                with act.Fori(0, blocks) as i:
                    for c in range(CT):
                        act.wait_ge(*banks.full(i, ("xT", c)))
                        act.activation(xT[:, c, :], banks.bank(("xT", c)), ACT.Copy, scale=ln2w[:, c:c + 1])\
                           .then_inc(banks.release(("xT", c)), 1)
                    act.wait_ge(*banks.full(i, ("z", 0)))
                    act.activation(zT[0:NR, :], banks.bank(("z", 0))[0:NR, :], ACT.Identity, bias=rb[:, 0:1])\
                       .then_inc(banks.release(("z", 0)), 1)
                    act.wait_ge(*banks.full(i, ("zT", 0)))
                    act.activation(half[:, :, :],
                                   banks.bank(("zT", 0)).rearrange("p (t n) -> p t n", t=TT)[:, :, 0:NR],
                                   ACT.Tanh, scale=0.5).then_inc(banks.release(("zT", 0)), 1)
                    for step in expert_order():
                        if step[0] == "GU":
                            _, e, m = step
                            n = e * FT + m
                            if n >= 2:
                                act.wait_ge(*banks.out(i, ("gate", *divmod(n - 2, FT))))
                            act.wait_ge(*banks.full(i, ("gate", e, m)))
                            act.activation(tanh[:, n % 2, :], banks.bank(("gate", e, m)), ACT.Tanh, scale=0.5)\
                               .then_inc(tanh_done.sem, 1)

            @block.vector
            def _(dve):
                dve.wait_ge(consts, N_CONSTS)

                def routing(i):
                    steps = [0]

                    def step(ins):
                        steps[0] += 1
                        ins.then_inc(route_step.sem, 1)

                    def so_far():
                        dve.wait_ge(*route_step.after(i, steps[0]))
                        dve.sem_inc(dve_turn, 1)

                    dve.wait_ge(*banks.out(i, ("zT", 0)))
                    dve.tensor_scalar(chance[:, :, 0:NR], half[:, :, :], 0.5, 0.5, ALU.mult, ALU.add)\
                       .then_inc(chance_done.sem, 1)
                    dve.wait_ge(*chance_done.after(i, 1))
                    dve.sem_inc(dve_turn, 1)
                    for t in range(TT):
                        step(dve.max(best[:, t, :], chance[:, t, :]))
                    so_far()
                    for t in range(TT):
                        step(dve.max_index(where[:, t, :], best[:, t, :], chance[:, t, :]))
                    step(dve.tensor_tensor(den[:, :], best[:, :, 0], best[:, :, 1], ALU.add))
                    so_far()
                    step(dve.reciprocal(rden[:, :], den[:, :]))
                    step(dve.tensor_copy(wheref[:, :, :], where[:, :, 0:2]))
                    so_far()
                    step(dve.tensor_tensor(share[:, :, :], best[:, :, 0:2],
                                           rden[:, :].unsqueeze(2).to_broadcast([P, TT, 2]), ALU.mult))
                    so_far()
                    for s in range(2):
                        for t in range(TT):
                            step(dve.tensor_scalar(part[:, s, t, :], number[:, :], wheref[:, t, s:s + 1],
                                                   share[:, t, s:s + 1], ALU.is_equal, ALU.mult))
                    so_far()
                    step(dve.tensor_tensor(gain[:, :, :], part[:, 0], part[:, 1], ALU.add))
                    so_far()
                    assert steps[0] == ROUTE

                def activate(i, e, m):
                    n = e * FT + m
                    dve.wait_ge(*tanh_done.after(i, n + 1))
                    dve.scalar_tensor_tensor(out=gated[:, n % 2, :], in0=tanh[:, n % 2, :], scalar=1.0,
                                             in1=banks.bank(("gate", e, m)), op0=ALU.add, op1=ALU.mult)\
                       .then_inc(banks.release(("gate", e, m)), 1)
                    dve.wait_ge(*banks.out(i, ("gate", e, m)))
                    dve.wait_ge(*banks.full(i, ("up", e, m)))
                    dve.scalar_tensor_tensor(out=actT[:, e % 2, m, :], in0=gated[:, n % 2, :], scalar=1.0 / 16.0,
                                             in1=banks.bank(("up", e, m)), op0=ALU.mult, op1=ALU.mult)\
                       .then_inc(banks.release(("up", e, m)), 1)

                def add_expert(i, e):
                    for t in range(TT):
                        name = ("down", e, t)
                        dve.wait_ge(*banks.full(i, name))
                        if e == 0:
                            ins = dve.tensor_tensor(h[:, 0, t, :], banks.bank(name), h[:, 0, t, :], ALU.add)
                        else:
                            dve.wait_ge(*banks.out(i, ("down", e - 1, t)))
                            ins = dve.scalar_tensor_tensor(out=h[:, 0, t, :], in0=banks.bank(name),
                                                           scalar=gain[:, t, e - 1:e], in1=h[:, 0, t, :],
                                                           op0=ALU.mult, op1=ALU.add)
                        ins.then_inc(banks.release(name), 1)

                with dve.Fori(0, blocks) as i:
                    dve.wait_ge(*h_loaded.after(i, 16))
                    for t in range(TT):
                        dve.tensor_tensor_reduce(unused[:, t, :], h[:, 0, t, :], h[:, 0, t, :], 1.0 / D, 0.0,
                                                 ALU.mult, ALU.add, square[:, t:t + 1]).then_inc(squared.sem, 1)
                    dve.wait_ge(*rms_done.after(i, 1))
                    for t in range(TT):
                        dve.tensor_scalar(xr[:, t, :], h[:, 0, t, :], rms[:, t:t + 1], None, ALU.mult)\
                           .then_inc(xr_done.sem, 1)
                    routing(i)
                    for step in expert_order():
                        if step[0] == "GU":
                            activate(i, *step[1:])
                        else:
                            add_expert(i, step[1])
                    for t in range(TT):
                        dve.wait_ge(*banks.out(i, ("down", NE - 1, t)))
                        dve.bn_stats(stats[:, t, :], h[:, 0, t, :]).then_inc(stats_done.sem, 1)
                    for t in range(TT):
                        dve.wait_ge(*stats_done.after(i, t + 1))
                        dve.sem_inc(dve_turn, 1)
                        dve.bn_aggr(meanvar[:, t, :], stats[:, t, :]).then_inc(meanvar_done.sem, 1)
                    dve.wait_ge(*rstd_done.after(i, 1))
                    for t in range(TT):
                        dve.tensor_scalar(xr[:, t, :], h[:, 0, t, :], meanvar[:, t, 0:1], rstd[:, t:t + 1],
                                          ALU.subtract, ALU.mult).then_inc(closed.sem, 1)
                    dve.wait_ge(*x1_loaded.after(i, 16))
                    for t in range(TT):
                        dve.wait_ge(*closed.after(i, t + 1))
                        dve.tensor_tensor(x1[:, 0, t, :], xr[:, t, :], x1[:, 0, t, :], ALU.add)\
                           .then_inc(out_ready.sem, 1)

            @block.tensor
            def _(pe):
                pe.wait_ge(consts, N_CONSTS)
                pe.wait_ge(small_in, 16 * N_SMALL)
                def product(to, pairs):
                    for n, (left, right) in enumerate(pairs):
                        ins = pe.matmul(to, left, right, start=(n == 0), stop=(n == len(pairs) - 1))
                    return ins

                with pe.Fori(0, blocks) as i:
                    pe.wait_ge(*xr_done.after(i, TT))
                    for c in range(CT):
                        to = banks.bank(("xT", c))
                        pe.wait_ge(*banks.empty(i, ("xT", c)))
                        for t in range(TT):
                            ins = pe.transpose(to[:, t * P:(t + 1) * P], xr[:, t, c * P:(c + 1) * P], ident[:, :])
                        ins.then_inc(filled, 1)
                    to = banks.bank(("z", 0))
                    pe.wait_ge(*banks.empty(i, ("z", 0)))
                    for c in range(CT):
                        pe.wait_ge(*banks.out(i, ("xT", c)))
                    product(to[0:NR, :], [(wr[:, c, :], xT[:, c, :]) for c in range(CT)]).then_inc(filled, 1)
                    to = banks.bank(("zT", 0))
                    pe.wait_ge(*banks.empty(i, ("zT", 0)))
                    pe.wait_ge(*banks.out(i, ("z", 0)))
                    for t in range(TT):
                        ins = pe.transpose(to[:, t * P:(t + 1) * P], zT[:, t * P:(t + 1) * P], ident[:, :])
                    ins.then_inc(filled, 1)
                    for step in expert_order():
                        if step[0] == "GU":
                            _, e, m = step
                            pe.wait_ge(expert_in[e], 48)
                            for name, w in (("gate", wg), ("up", wu)):
                                to = banks.bank((name, e, m))
                                pe.wait_ge(*banks.empty(i, (name, e, m)))
                                product(to, [(w[:, e, c, m * P:(m + 1) * P], xT[:, c, :]) for c in range(CT)])\
                                    .then_inc(filled, 1)
                        else:
                            e = step[1]
                            for m in range(FT):
                                pe.wait_ge(*banks.out(i, ("up", e, m)))
                            for t in range(TT):
                                to = banks.bank(("down", e, t))
                                pe.wait_ge(*banks.empty(i, ("down", e, t)))
                                product(to, [(actT[:, e % 2, m, t * P:(t + 1) * P], wd[:, e, m, :])
                                             for m in range(FT)]).then_inc(filled, 1)


def build(nc, a, out, blocks):
    kept = [nc.dram_tensor(name, (blocks, T, D), F32, kind="Internal").ap() for name in ("x1_kept", "h_kept")]
    attention_layers(nc, a["L0_attn_x"],
                     [a[n] for n in ("L0_attn_w_qkv", "L0_attn_w_o")] +
                     [a[f"L0_ffn_{n}"] for n in ("kv_d_w", "q_d_w", "k_u_w", "v_u_w", "q_u_w", "rope_k_w",
                                                 "rope_q_w", "o_w")],
                     (a["rope1"], a["rope2"]), a["L0_ffn_ln1_w"], kept[0], kept[1], blocks)
    expert_layer(nc, kept[1], kept[0], a["L0_ffn_ln2_w"],
                 [a[f"L0_ffn_{n}"] for n in ("sh_gate", "sh_up", "sh_down", "r_gate", "r_up", "r_down",
                                             "router_w", "router_b")], out, blocks)


def rope_table(width):
    inverse = (np.float32(1.0) / np.float32(10000.0) ** (np.arange(0, width, 2, dtype=np.float32) / np.float32(width)))
    angle = np.outer(np.arange(T, dtype=np.float32), inverse.astype(np.float32)).astype(np.float32)
    cos, sin = np.cos(angle), np.sin(angle)
    table = np.stack([np.concatenate([cos, cos], 1), np.concatenate([-sin, sin], 1)], 1)
    return np.ascontiguousarray(table.reshape(TT, P, 2, width).transpose(1, 0, 2, 3).astype(np.float32))


def kernel(**inputs):
    import concourse.bacc as bacc
    from concourse.bass_utils import run_bass_kernel_spmd

    nc = bacc.Bacc("TRN2", target_bir_lowering=False, num_devices=1)
    arrays, a = {}, {}
    tables = {"rope1": rope_table(HD), "rope2": rope_table(RD)}
    for name, value in {**inputs, **tables}.items():
        if name in ("L0_ffn_ln1_w", "L0_ffn_ln2_w"):
            value = np.asarray(value).reshape(CT, P).T
        if name == "L0_ffn_router_b":
            value = np.asarray(value).reshape(NR, 1)
        value = np.ascontiguousarray(value)
        arrays[f"in_{name}"] = value
        a[name] = nc.dram_tensor(f"in_{name}", value.shape, mybir.dt.from_np(value.dtype), kind="ExternalInput").ap()
    blocks = inputs["L0_attn_x"].shape[0]
    out = nc.dram_tensor("out", (blocks, T, D), F32, kind="ExternalOutput").ap()
    build(nc, a, out, blocks)
    result = run_bass_kernel_spmd(nc, [arrays], core_ids=[0])
    return result.results[0]["out"]
```

```python
from contextlib import ExitStack

import numpy as np

import concourse.bass as bass
from concourse import mybir

F32 = mybir.dt.float32
F32R = mybir.dt.float32r
BF16 = mybir.dt.bfloat16
U32 = mybir.dt.uint32
ALU = mybir.AluOpType
ACT = mybir.ActivationFunctionType

P = 128
D = 512
CT = D // P
T = 512
TT = T // P
NH = 16
HD = D // NH
GH = P // HD
NG = NH // GH
RD = HD // 2
LAT = D // 4
FF = 256
FT = FF // P
NR = 7
NE = NR + 1
EPS = 1e-5
SCALE = float(HD) ** -0.5
MASKED = -3.0e38
ROWMAX = 3 * HD
STACKS = 3


class Signal:

    def __init__(self, sem, per_pass):
        self.sem, self.per_pass = sem, per_pass

    def after(self, i, k):
        return self.sem, i * self.per_pass + (k + 1)


class Banks:

    def __init__(self, tensor, filled, freed, names):
        self.tensor, self.filled, self.freed = tensor, filled, freed
        self.n = len(freed)
        assert len(names) % self.n == 0 and len(set(names)) == len(names)
        self.number = {name: k for k, name in enumerate(names)}
        self.per_pass = len(names)

    def at(self, name):
        return self.number[name] % self.n

    def bank(self, name):
        return self.tensor[:, self.at(name), :]

    def full(self, i, name):
        return self.filled, i * self.per_pass + (self.number[name] + 2)

    def empty(self, i, name):
        return self.freed[self.at(name)], i * (self.per_pass // self.n) + (self.number[name] // self.n + 1)

    def out(self, i, name):
        return self.freed[self.at(name)], i * (self.per_pass // self.n) + (self.number[name] // self.n + 2)

    def release(self, name):
        return self.freed[self.at(name)]


def attention_order(a):
    if a == 0:
        yield from [("P", 0, 0), ("P", 0, 1), ("P", 1, 0), ("T", 0, 0), ("P", 1, 1), ("V", 0, 0), ("V", 1, 0),
                    ("T", 1, 0), ("V", 2, 0), ("S", 0, 0), ("V", 3, 0), ("S", 0, 1), ("S", 0, 2), ("S", 0, 3),
                    ("P", 2, 0), ("M", 0, 0), ("P", 2, 1)]
    else:
        yield from [("P", 0, 0), ("P", 0, 1), ("P", 1, 0), ("P", 1, 1), ("T", 0, 0), ("V", 0, 0), ("V", 1, 0),
                    ("V", 2, 0), ("V", 3, 0), ("P", 2, 0), ("P", 2, 1), ("T", 1, 0), ("S", 0, 0), ("S", 0, 1),
                    ("S", 0, 2), ("S", 0, 3), ("M", 0, 0)]
    for g in range(NG):
        last = g == NG - 1
        yield "ST", g, 0
        if not last:
            yield from [("S", g + 1, 0), ("S", g + 1, 1)]
        yield "ST", g, 1
        if last:
            yield "Y", 0, 0
        if a == 1 and last:
            yield "R", 0, 0
        if g + 2 < NG:
            yield "T", g + 2, 0
        if not last:
            yield "S", g + 1, 2
        yield "PV", g, 0
        if g == 0:
            yield "P", 3, 0
        if not last:
            yield "S", g + 1, 3
        if a == 1 and g == NG - 2:
            yield from [("L", t, 0) for t in range(TT)]
        yield "ST", g, 2
        if not last:
            yield "M", g + 1, 0
        if g == 0:
            yield "P", 3, 1
        if a == 1 and last:
            yield from [("N", t, 0) for t in range(TT)]
        yield "PV", g, 1
        yield "ST", g, 3
        yield "PV", g, 2
        yield "PV", g, 3
    yield from [("Y", 1, 0), ("Y", 0, 1), ("Y", 1, 1), ("Y", 2, 0), ("Y", 2, 1), ("Y", 3, 0), ("Y", 3, 1)]


def attention_fills(a):
    for step, g, h in attention_order(a):
        if step == "P":
            yield ("q", "k")[h], a, g
        if step == "T":
            yield from [("qT", a, g), ("kT", a, g)]
        if step == "V":
            yield "v", a, g
        if step == "S":
            yield from [("S", a, g, h, part) for part in range(3)]
        if step == "M":
            yield "M", a, g
        if step == "Y" and h == 0:
            yield "y", a, g


def loop1_fills():
    names = [("xT", c) for c in range(CT)]
    names += attention_fills(0)
    names += [("xrT", c) for c in range(CT)]
    names += [("lat", m) for m in range(2)]
    names += attention_fills(1)
    return names

def loop2_fills():
    names = [("xT", c) for c in range(CT)] + [("z", 0), ("zT", 0)]
    for step in expert_order():
        if step[0] == "GU":
            names += [("gate", *step[1:]), ("up", *step[1:])]
        else:
            names += [("down", step[1], t) for t in range(TT)]
    return names


def expert_order():
    for e in range(NE):
        yield "GU", e, 0
        if e:
            yield "D", e - 1
        yield "GU", e, 1
    yield "D", NE - 1


def attention_layers(nc, x, weights, tables, ln1_w, x1_out, h_out, blocks):
    w_qkv, w_o, kv_d, q_d, k_u, v_u, q_u, rope_k, rope_q, o_w = weights
    with ExitStack() as ctx:
        signals = []

        def sb(name, shape, dt=F32):
            return ctx.enter_context(nc.sbuf_tensor(name, shape, dt))

        def semaphore(name):
            return ctx.enter_context(nc.semaphore(name))

        def signal(name, per_pass):
            signals.append(Signal(semaphore(name), per_pass))
            return signals[-1]

        wqkv = sb("wqkv", [P, CT, 3 * D])
        wo = sb("wo", [P, 2, CT, D])
        wlat = sb("wlat", [P, CT, 2, LAT])
        wku = sb("wku", [P, NH * RD])
        wvu = sb("wvu", [P, D])
        wq2 = sb("wq2", [P, NH, 2, RD])
        wkr = sb("wkr", [P, CT, NH * RD])
        rope1 = sb("rope1", [P, TT, 2, HD])
        rope2 = sb("rope2", [P, TT, 2, RD])
        ln1w = sb("ln1w", [P, CT])
        ident = sb("ident", [P, P])
        ones = sb("ones", [P, HD])
        minus_half = sb("minus_half", [P, TT])
        mask = sb("mask", [P, T])

        x_in = sb("x_in", [P, TT, D])
        x1 = sb("x1", [P, TT, D])
        xin = sb("xin", [P, TT, D])
        y = sb("y", [P, TT, D])
        xT = sb("xT", [P, CT, T])
        v = sb("v", [P, TT, D])
        latT = sb("latT", [P, 2, T])
        qk = sb("qk", [P, 2, 2, TT, P])
        turned = sb("turned", [P, 2, 2, T])
        parts = sb("parts", [P, 4, T], F32R)
        stacks = [sb(f"stacks{n}", [P, 2, GH, T], F32R) for n in range(STACKS)]
        probs = sb("probs", [P, 2, GH, T])
        total = sb("total", [P, T])
        unused = sb("unused", [P, TT, T], BF16)
        rowmax = sb("rowmax", [P, 2, GH * TT])
        negmax = sb("negmax", [GH * TT, 2, P], F32R)
        stats = sb("stats", [P, 3, TT, 6])
        meanvar = sb("meanvar", [P, 3, TT, 2])
        padded = sb("padded", [P, 3, TT, 2])
        rstd = sb("rstd", [P, 3, TT, 2])

        ring = ctx.enter_context(nc.psum_tensor("ring", [P, 2, 512], F32))
        scoresT = ctx.enter_context(nc.psum_tensor("scoresT", [P, 2, 2, 512], F32))
        out_ps = ctx.enter_context(nc.psum_tensor("out_ps", [P, 512], F32))
        sum_ps = ctx.enter_context(nc.psum_tensor("sum_ps", [P, 512], F32))

        names = loop1_fills()
        filled = semaphore("ring_filled")
        freed = [semaphore(f"ring_freed{n}") for n in range(2)]
        banks = Banks(ring, filled, freed, names)

        qkv_in = semaphore("qkv_in")
        rest_in = semaphore("rest_in")
        N_REST = 11
        consts = semaphore("consts")
        consts_step = semaphore("consts_step")
        N_CONSTS = 4 + STACKS
        pool_turn, dve_turn, sp_turn, act_turn = (semaphore(f"{e}_turn") for e in ("pool", "dve", "sp", "act"))
        x_loaded = signal("x_loaded", 16)
        first_normed = signal("first_normed", TT)
        stats_done = [signal(f"stats_done{n}", TT) for n in range(3)]
        meanvar_done = [signal(f"meanvar_done{n}", TT) for n in range(3)]
        padded_done = [signal(f"padded_done{n}", (1, TT, 2 * TT)[n]) for n in range(3)]
        rstd_done = [signal(f"rstd_done{n}", TT if n else 1) for n in range(3)]
        y_normed = signal("y_normed", TT)
        x1_done = signal("x1_done", TT)
        xin_done = signal("xin_done", TT)
        xr_done = signal("xr_done", TT)
        x1_stored = signal("x1_stored", 16)
        h_stored = signal("h_stored", 16)
        cos_done = signal("cos_done", 4 * NG)
        rotated = signal("rotated", 4 * NG)
        plain_done = signal("plain_done", 2 * NG)
        high_done = signal("high_done", 2 * 2 * NG)
        PER_STACK = 3 * GH * 16
        stacked = [signal(f"stacked{n}", PER_STACK) for n in range(2 * NG)]
        negmax_in = [signal(f"negmax_in{n}", NG * 16) for n in range(2)]
        max_done = signal("max_done", 2 * NH)
        st_filled = signal("st_filled", 2 * NG * TT * 2)
        exp_done = signal("exp_done", 2 * NG * TT * 2)
        causal = signal("causal", 2 * NG * TT)
        pv_done = signal("pv_done", 2 * NG * TT)
        total_done = signal("total_done", 2 * NG)
        out_done = signal("out_done", 2 * NG)

        with nc.Block() as block:
            @block.sync
            def _(sp):
                for s in signals:
                    sp.sem_inc(s.sem, 1)
                for sem in [filled, *freed]:
                    sp.sem_inc(sem, 1)

        with nc.Block() as block:

            @block.sync
            def _(sp):
                in_rows = "o (t p) c -> p (o t) c"
                by_c = "(c p) n -> p c n"
                sp.dma_start(x_in[:, :, :], x[0:1, :, :].rearrange(in_rows, p=P)).then_inc(x_loaded.sem, 16)
                sp.dma_start(rope1[:, :, :, :], tables[0]).then_inc(qkv_in, 16)
                sp.dma_start(wqkv[:, :, :], w_qkv.rearrange(by_c, p=P)).then_inc(qkv_in, 16)
                sp.dma_start(wo[:, 0], w_o.rearrange(by_c, p=P)).then_inc(rest_in, 16)
                sp.dma_start(rope2[:, :, :, :], tables[1]).then_inc(rest_in, 16)
                sp.dma_start(ln1w[:, :], ln1_w).then_inc(rest_in, 16)
                sp.dma_start(wlat[:, :, 0, :], kv_d.rearrange(by_c, p=P)).then_inc(rest_in, 16)
                sp.dma_start(wlat[:, :, 1, :], q_d.rearrange(by_c, p=P)).then_inc(rest_in, 16)
                sp.dma_start(wku[:, :], k_u).then_inc(rest_in, 16)
                sp.dma_start(wvu[:, :], v_u).then_inc(rest_in, 16)
                sp.dma_start(wq2[:, :, 0, :], q_u.rearrange("p (h d) -> p h d", h=NH)).then_inc(rest_in, 16)
                sp.dma_start(wq2[:, :, 1, :], rope_q.rearrange("p (h d) -> p h d", h=NH)).then_inc(rest_in, 16)
                sp.dma_start(wkr[:, :, :], rope_k.rearrange(by_c, p=P)).then_inc(rest_in, 16)
                sp.dma_start(wo[:, 1], o_w.rearrange(by_c, p=P)).then_inc(rest_in, 16)
                sp.wait_ge(consts, N_CONSTS)

                def stack(i, a, g):
                    n = a * NG + g
                    sp.wait_ge(*high_done.after(i, 2 * (n + 1)))
                    sp.sem_inc(sp_turn, 1)
                    sp.wait_ge(*banks.out(i, ("qT", a, g)))
                    sp.sem_inc(sp_turn, 1)
                    sp.wait_ge(*banks.out(i, ("kT", a, g)))
                    sp.sem_inc(sp_turn, 1)
                    sp.wait_ge(*st_filled.after(i, max(0, 2 * TT * (n - STACKS + 1))))
                    sp.sem_inc(sp_turn, 1)
                    for s, chosen in enumerate((slice(0, 2), slice(2, 0, -1), slice(0, 4, 3))):
                        for h in range(GH):
                            sp.dma_start(stacks[n % STACKS][s * HD:(s + 1) * HD, :, h, :].bitcast(F32),
                                         parts[h * HD:(h + 1) * HD, chosen, :].bitcast(F32))\
                              .then_inc(stacked[n].sem, 16)

                with sp.Fori(0, blocks) as i:
                    for g in range(NG):
                        stack(i, 0, g)
                    sp.wait_ge(*x1_done.after(i, TT))
                    sp.sem_inc(sp_turn, 1)
                    sp.dma_start(x1_out[bass.ds(i, 1), :, :].rearrange(in_rows, p=P), x1[:, :, :])\
                      .then_inc(x1_stored.sem, 16)
                    sp.dma_start(x_in[:, :, :], x[bass.ds((i + 1) % blocks, 1), :, :].rearrange(in_rows, p=P))\
                      .then_inc(x_loaded.sem, 16)
                    for g in range(NG):
                        stack(i, 1, g)
                    for t in range(TT - 2, TT):
                        sp.wait_ge(*banks.out(i, ("y", 1, t)))
                        sp.sem_inc(sp_turn, 1)
                    sp.dma_start(h_out[bass.ds(i, 1), :, :].rearrange(in_rows, p=P), y[:, :, :])\
                      .then_inc(h_stored.sem, 16)
                sp.wait_ge(*x1_stored.after(blocks - 1, 16))
                sp.wait_ge(*h_stored.after(blocks - 1, 16))
                sp.wait_ge(*x_loaded.after(blocks - 1, 32))

            @block.gpsimd
            def _(pool):
                pool.memset(ones[:, :], 1.0).then_inc(consts, 1)
                pool.memset(minus_half[:, :], -0.5).then_inc(consts, 1)
                pool.memset(ident[:, :], 0.0).then_inc(consts_step, 1)
                pool.memset(mask[:, :], 0.0).then_inc(consts_step, 1)
                pool.wait_ge(consts_step, 2)
                pool.affine_select(out=ident[:, :], in_=ident[:, :], compare_op=ALU.not_equal, fill=1.0,
                                   base=0, pattern=[[-1, P]], channel_multiplier=1).then_inc(consts, 1)
                pool.affine_select(out=mask[:, :], in_=mask[:, :], compare_op=ALU.is_ge, fill=MASKED,
                                   base=T - P, pattern=[[-1, T]], channel_multiplier=1).then_inc(consts, 1)

                def first_roots(i, before):
                    pool.wait_ge(*meanvar_done[0].after(i, before + TT))
                    pool.sem_inc(pool_turn, 1)
                    pool.tensor_scalar(padded[:, 0, :, 0], meanvar[:, 0, :, 1], EPS, None, ALU.add)\
                        .then_inc(padded_done[0].sem, 1)
                    pool.wait_ge(*padded_done[0].after(i, before // TT + 1))
                    pool.tensor_tensor(rstd[:, 0, :, 0], padded[:, 0, :, 0], minus_half[:, 0:TT], ALU.pow)\
                        .then_inc(rstd_done[0].sem, 1)

                def y_root(i, t):
                    pool.wait_ge(*meanvar_done[1].after(i, t + 1))
                    pool.sem_inc(pool_turn, 1)
                    pool.tensor_scalar(padded[:, 1, t, 0:1], meanvar[:, 1, t, 1:2], EPS, None, ALU.add)\
                        .then_inc(padded_done[1].sem, 1)
                    pool.wait_ge(*padded_done[1].after(i, t + 1))
                    pool.tensor_tensor(rstd[:, 1, t, 0:1], padded[:, 1, t, 0:1], minus_half[:, 0:1], ALU.pow)\
                        .then_inc(rstd_done[1].sem, 1)

                def x1_roots(i, t):
                    pool.wait_ge(*meanvar_done[2].after(i, t + 1))
                    pool.sem_inc(pool_turn, 1)
                    pool.tensor_scalar(padded[:, 2, t, 0:1], meanvar[:, 2, t, 1:2], EPS, None, ALU.add)\
                        .then_inc(padded_done[2].sem, 1)
                    pool.tensor_scalar(padded[:, 2, t, 1:2], meanvar[:, 2, t, 1:2], 1.0 + EPS, EPS * EPS,
                                       ALU.mult, ALU.add).then_inc(padded_done[2].sem, 1)
                    pool.wait_ge(*padded_done[2].after(i, 2 * (t + 1)))
                    pool.tensor_tensor(rstd[:, 2, t, :], padded[:, 2, t, :], minus_half[:, 0:2], ALU.pow)\
                        .then_inc(rstd_done[2].sem, 1)

                def add_rotated(i, a, g, which):
                    r = 2 * (a * NG + g) + which
                    pool.wait_ge(*cos_done.after(i, r + 1))
                    pool.wait_ge(*banks.out(i, (("q", "k")[which], a, g)))
                    if g >= 2:
                        pool.sem_inc(pool_turn, 1)
                        pool.wait_ge(*banks.full(i, ("kT", a, g - 2)))
                    if a == 0:
                        pool.tensor_tensor(qk[:, g % 2, which, :, :].rearrange("p t d -> p (t d)"),
                                           turned[:, r % 2, 0, :], turned[:, r % 2, 1, :], ALU.add)\
                            .then_inc(rotated.sem, 1)
                    else:
                        rows = qk[:, g % 2, which, :, :].rearrange("p t (h s d) -> p (t h) s d", h=GH, s=2)
                        cos_part, sin_part = (turned[:, r % 2, s, 0:T // 2].rearrange("p (t d) -> p t d", d=RD)
                                              for s in range(2))
                        pool.tensor_tensor(rows[:, :, 1, :], cos_part, sin_part, ALU.add).then_inc(rotated.sem, 1)

                def cut(i, n):
                    pool.wait_ge(*exp_done.after(i, 2 * (n + 1)))
                    pool.sem_inc(pool_turn, 1)
                    diagonal = probs[:, n % 2, :, 0:P]
                    pool.affine_select(out=diagonal, in_=diagonal, compare_op=ALU.is_ge, fill=0.0,
                                       base=0, pattern=[[0, GH], [1, P]], channel_multiplier=-1)\
                        .then_inc(causal.sem, 1)

                def attend(i, a):
                    for step, g, h in attention_order(a):
                        if step == "P":
                            add_rotated(i, a, g, h)
                        if step == "ST":
                            cut(i, (a * NG + g) * TT + h)
                        if step == "R":
                            first_roots(i, TT)

                pool.wait_ge(consts, N_CONSTS)
                first_roots(0, 0)
                with pool.Fori(0, blocks) as i:
                    attend(i, 0)
                    for step, t in norm_order():
                        if step == "A":
                            y_root(i, t)
                        if step == "B":
                            x1_roots(i, t)
                    attend(i, 1)

            @block.scalar
            def _(act):

                def copy(i, name, to, scale=1.0):
                    act.wait_ge(*banks.full(i, name))
                    act.activation(to, banks.bank(name), ACT.Copy, scale=scale)\
                       .then_inc(banks.release(name), 1)

                def take_high(i, a, g):
                    n = a * NG + g
                    if n > 0:
                        act.wait_ge(*stacked[n - 1].after(i, PER_STACK))
                    else:
                        act.wait_ge(*stacked[2 * NG - 1].after(i, 0))
                    for which, name in enumerate(("qT", "kT")):
                        act.wait_ge(*banks.full(i, (name, a, g)))
                        act.activation(parts[:, which, :], banks.bank((name, a, g)), ACT.Copy)\
                           .then_inc(high_done.sem, 1)

                def take_negmax(i, a, g):
                    n = a * NG + g
                    act.wait_ge(*negmax_in[n % 2].after(i, 16 * (n // 2)))
                    act.wait_ge(*banks.full(i, ("M", a, g)))
                    act.activation(negmax[:, n % 2, :], banks.bank(("M", a, g))[0:GH * TT, 0:P], ACT.Copy,
                                   scale=-1.0).then_inc(banks.release(("M", a, g)), 1)
                    act.wait_ge(*banks.out(i, ("M", a, g)))
                    act.sem_inc(act_turn, 1)
                    act.dma_start(stacks[n % STACKS][ROWMAX:ROWMAX + 1, 0, :, :].rearrange("o h t -> o (h t)")
                                  .bitcast(F32), negmax[:, n % 2, :].bitcast(F32)).then_inc(negmax_in[n % 2].sem, 16)

                def exps(i, a, g, j):
                    m = (a * NG + g) * TT + j
                    act.wait_ge(*pv_done.after(i, max(0, m - 1)))
                    first, width = (P, P) if j == TT - 1 else (0, T - P * j)
                    for pair in range(2):
                        u = 2 * m + pair
                        act.wait_ge(*st_filled.after(i, u + 1))
                        act.activation(probs[:, m % 2, 2 * pair:2 * pair + 2, 0:width],
                                       scoresT[:, u % 2, :, first:first + width], ACT.Exp, scale=SCALE)\
                           .then_inc(exp_done.sem, 1)

                def attend(i, a):
                    for step, g, h in attention_order(a):
                        if step == "T":
                            take_high(i, a, g)
                        if step == "V":
                            copy(i, ("v", a, g), v[:, g, :])
                        if step == "M":
                            take_negmax(i, a, g)
                        if step == "ST":
                            exps(i, a, g, h)
                        if step == "Y" and h == 1 and a == 0:
                            act.wait_ge(*h_stored.after(i, 0))
                            copy(i, ("y", 0, g), y[:, g, :])

                act.wait_ge(rest_in, 16 * N_REST)
                act.wait_ge(consts, N_CONSTS)
                with act.Fori(0, blocks) as i:
                    for c in range(CT):
                        copy(i, ("xT", c), xT[:, c, :])
                    attend(i, 0)
                    for c in range(CT):
                        copy(i, ("xrT", c), xT[:, c, :], scale=ln1w[:, c:c + 1])
                    for m in range(2):
                        copy(i, ("lat", m), latT[:, m, :])
                    attend(i, 1)

            @block.vector
            def _(dve):
                for n in range(STACKS):
                    dve.memset(stacks[n][ROWMAX:ROWMAX + 1, 1, :, :].bitcast(F32), 1.0).then_inc(consts, 1)
                dve.wait_ge(consts, N_CONSTS)

                def take_stats(i, m, t, rows, before=0):
                    dve.bn_stats(stats[:, m, t, :], rows[:, t, :]).then_inc(stats_done[m].sem, 1)
                    dve.wait_ge(*stats_done[m].after(i, before + t + 1))
                    dve.sem_inc(dve_turn, 1)
                    dve.bn_aggr(meanvar[:, m, t, :], stats[:, m, t, :]).then_inc(meanvar_done[m].sem, 1)

                def norm(to, rows, m, t, s, done):
                    dve.tensor_scalar(to[:, t, :], rows[:, t, :], meanvar[:, m, t, 0:1], rstd[:, m, t, s:s + 1],
                                      ALU.subtract, ALU.mult).then_inc(done.sem, 1)

                def rotate(i, a, g, which):
                    r = 2 * (a * NG + g) + which
                    name = ("q", "k")[which], a, g
                    dve.wait_ge(*banks.full(i, name))
                    if a == 0:
                        rows = banks.bank(name).rearrange("p (t h d) -> p t h d", t=TT, h=GH)
                    else:
                        split = "p (t h s d) -> p t h s d" if which == 0 else "p (t s h d) -> p t h s d"
                        halves = banks.bank(name).rearrange(split, t=TT, h=GH, s=2)
                        to = qk[:, g % 2, which, :, :].rearrange("p t (h s d) -> p t h s d", h=GH, s=2)
                        if g >= 2:
                            dve.sem_inc(dve_turn, 1)
                            dve.wait_ge(*banks.full(i, ("kT", a, g - 2)))
                        dve.tensor_copy(to[:, :, :, 0, :], halves[:, :, :, 0, :]).then_inc(plain_done.sem, 1)
                        rows = halves[:, :, :, 1, :]
                    dve.wait_ge(*rotated.after(i, max(0, r - 1)))
                    width, table = ((HD, rope1), (RD, rope2))[a]
                    cos_part, sin_part = (turned[:, r % 2, s, 0:TT * GH * width]
                                          .rearrange("p (t h d) -> p t h d", t=TT, h=GH) for s in range(2))
                    cos, sin = (table[:, :, s, :].unsqueeze(2).to_broadcast([P, TT, GH, width]) for s in range(2))
                    dve.tensor_tensor(cos_part, rows, cos, ALU.mult).then_inc(cos_done.sem, 1)
                    first, second = slice(0, width // 2), slice(width // 2, width)
                    dve.tensor_tensor(sin_part[:, :, :, first], rows[:, :, :, second], sin[:, :, :, first], ALU.mult)
                    dve.tensor_tensor(sin_part[:, :, :, second], rows[:, :, :, first], sin[:, :, :, second], ALU.mult)\
                       .then_inc(banks.release(name), 1)

                def take_low(i, a, g):
                    n = a * NG + g
                    for which, name in enumerate(("qT", "kT")):
                        dve.wait_ge(*high_done.after(i, 2 * n + which + 1))
                        dve.tensor_tensor(parts[:, 2 + which, :], banks.bank((name, a, g)), parts[:, which, :],
                                          ALU.subtract).then_inc(banks.release((name, a, g)), 1)

                def maxima(i, a, g, h):
                    n = a * NG + g
                    before = divmod(GH * n + h - 1, GH)
                    for t in range(TT):
                        name = ("S", a, g, h, max(0, t - 1))
                        first = P * 2 * (t == 1)
                        dve.wait_ge(*banks.full(i, name))
                        if t == 0 or before[0] < 0:
                            dve.wait_ge(*max_done.after(i, GH * n + h))
                        else:
                            dve.wait_ge(*banks.out(i, ("S", *divmod(before[0], NG), before[1], t - 1)))
                        dve.sem_inc(dve_turn, 1)
                        width = P * (t + 1)
                        ins = dve.tensor_tensor_reduce(
                            unused[:, t, 0:width], banks.bank(name)[:, first:first + width],
                            mask[:, T - width:T], 1.0, MASKED, ALU.add, ALU.max,
                            rowmax[:, n % 2, TT * h + t:TT * h + t + 1])
                        if t == 0:
                            ins.then_inc(max_done.sem, 1)
                        else:
                            ins.then_inc(banks.release(name), 1)

                def close(i, a, g):
                    n = a * NG + g
                    dve.wait_ge(*pv_done.after(i, TT * (n + 1)))
                    dve.reciprocal(total[:, :], sum_ps[:, :]).then_inc(total_done.sem, 1)
                    dve.wait_ge(*total_done.after(i, n + 1))
                    dve.tensor_tensor(xT[:, g, :], out_ps[:, :], total[:, :], ALU.mult)\
                       .then_inc(out_done.sem, 1)

                def attend(i, a):
                    for step, g, h in attention_order(a):
                        if step == "P":
                            rotate(i, a, g, h)
                        if step == "T":
                            take_low(i, a, g)
                        if step == "S":
                            if h == 0 and g >= 2:
                                dve.wait_ge(*banks.full(i, ("M", a, g - 2)))
                                dve.sem_inc(dve_turn, 1)
                            maxima(i, a, g, h)
                        if step == "PV" and h == TT - 1:
                            close(i, a, g)
                        if step == "L":
                            dve.wait_ge(*x_loaded.after(i, 32))
                            take_stats(i, 0, g, x_in, before=TT)
                        if step == "N":
                            dve.wait_ge(*rstd_done[0].after(i, 2))
                            dve.wait_ge(*x1_stored.after(i, 16))
                            norm(x1, x_in, 0, g, 0, first_normed)

                dve.wait_ge(*x_loaded.after(0, 16))
                for t in range(TT):
                    take_stats(0, 0, t, x_in)
                dve.wait_ge(*rstd_done[0].after(0, 1))
                for t in range(TT):
                    norm(x1, x_in, 0, t, 0, first_normed)
                dve.wait_ge(qkv_in, 32)
                dve.wait_ge(rest_in, 16 * N_REST)
                with dve.Fori(0, blocks) as i:
                    attend(i, 0)
                    for step, t in norm_order():
                        if step == "A":
                            dve.wait_ge(*banks.out(i, ("y", 0, t)))
                            take_stats(i, 1, t, y)
                        if step == "B":
                            dve.wait_ge(*rstd_done[1].after(i, t + 1))
                            norm(y, y, 1, t, 0, y_normed)
                            dve.wait_ge(*y_normed.after(i, t + 1))
                            dve.tensor_tensor(x1[:, t, :], y[:, t, :], x_in[:, t, :], ALU.add)\
                               .then_inc(x1_done.sem, 1)
                            dve.wait_ge(*x1_done.after(i, t + 1))
                            take_stats(i, 2, t, x1)
                        if step == "C":
                            dve.wait_ge(*rstd_done[2].after(i, t + 1))
                            norm(y, x1, 2, t, 1, xr_done)
                            norm(xin, x1, 2, t, 0, xin_done)
                    attend(i, 1)
                    for t in range(TT):
                        dve.wait_ge(*banks.full(i, ("y", 1, t)))
                        dve.tensor_tensor(y[:, t, :], banks.bank(("y", 1, t)), xin[:, t, :], ALU.add)\
                           .then_inc(banks.release(("y", 1, t)), 1)

            @block.tensor
            def _(pe):

                def product(to, pairs):
                    for n, (left, right) in enumerate(pairs):
                        ins = pe.matmul(to, left, right, start=(n == 0), stop=(n == len(pairs) - 1))
                    return ins

                def tile_of(rows_T, c, t):
                    return rows_T[:, c, t * P:(t + 1) * P]

                def transpose_columns(i, name, rows, c):
                    pe.wait_ge(*banks.empty(i, name))
                    for t in range(TT):
                        ins = pe.transpose(tile_of(ring, banks.at(name), t), rows[:, t, c * P:(c + 1) * P], ident[:, :])
                    ins.then_inc(filled, 1)

                def project(i, a, g, which):
                    name = ("q", "k")[which], a, g
                    pe.wait_ge(*banks.empty(i, name))
                    for t in range(TT):
                        to = tile_of(ring, banks.at(name), t)
                        if a == 0:
                            first = which * D + g * P
                            ins = product(to, [(tile_of(xT, c, t), wqkv[:, c, first:first + P]) for c in range(CT)])
                        elif which == 0:
                            ins = product(to, [(tile_of(latT, 1, t),
                                                wq2[:, g * GH:(g + 1) * GH, :, :].rearrange("p h s d -> p (h s d)"))])
                        else:
                            mine = slice(g * GH * RD, (g + 1) * GH * RD)
                            product(to[:, 0:GH * RD], [(tile_of(latT, 0, t), wku[:, mine])])
                            ins = product(to[:, GH * RD:P], [(tile_of(xT, c, t), wkr[:, c, mine]) for c in range(CT)])
                    ins.then_inc(filled, 1)

                def transpose_group(i, a, g):
                    n = a * NG + g
                    for which, name in enumerate(("qT", "kT")):
                        pe.wait_ge(*banks.empty(i, (name, a, g)))
                        pe.wait_ge(*rotated.after(i, 2 * n + which + 1))
                        if a == 1:
                            pe.wait_ge(*plain_done.after(i, 2 * g + which + 1))
                        for t in range(TT):
                            ins = pe.transpose(tile_of(ring, banks.at((name, a, g)), t),
                                               qk[:, g % 2, which, t, :], ident[:, :])
                        ins.then_inc(filled, 1)

                def values(i, a, t):
                    name = "v", a, t
                    pe.wait_ge(*banks.empty(i, name))
                    if a == 0:
                        pairs = [(tile_of(xT, c, t), wqkv[:, c, 2 * D:3 * D]) for c in range(CT)]
                    else:
                        pairs = [(tile_of(latT, 0, t), wvu[:, :])]
                    product(banks.bank(name), pairs).then_inc(filled, 1)

                def scores(i, a, g, h):
                    n = a * NG + g
                    heads = stacks[n % STACKS]
                    if h == 0:
                        pe.wait_ge(*stacked[n].after(i, PER_STACK))
                    for part, tiles in enumerate(((0, 1), (2,), (3,))):
                        name = "S", a, g, h, part
                        pe.wait_ge(*banks.empty(i, name))
                        for t in tiles:
                            width = max(2 * P, P * (t + 1))
                            first = 2 * P * (t == 1)
                            ins = pe.matmul(banks.bank(name)[:, first:first + width],
                                            heads[0:ROWMAX, 0, h, t * P:(t + 1) * P],
                                            heads[0:ROWMAX, 1, h, 0:width], start=True, stop=True)
                        ins.then_inc(filled, 1)

                def transpose_max(i, a, g):
                    n = a * NG + g
                    name = "M", a, g
                    pe.wait_ge(*banks.empty(i, name))
                    pe.wait_ge(*max_done.after(i, GH * (n + 1)))
                    last = "S", a, g, GH - 1, 2
                    if banks.at(last) != banks.at(name):
                        pe.wait_ge(*banks.out(i, last))
                    pe.transpose(banks.bank(name)[0:GH * TT, 0:P], rowmax[:, n % 2, :], ident[:, :]).then_inc(filled, 1)

                def scores_less_max(i, a, g, j):
                    n = a * NG + g
                    heads = stacks[n % STACKS]
                    if j == 0:
                        pe.wait_ge(*negmax_in[n % 2].after(i, 16 * (n // 2 + 1)))
                    first = min(P * j, T - 2 * P)
                    for pair in range(2):
                        u = 2 * (TT * n + j) + pair
                        pe.wait_ge(*exp_done.after(i, max(0, u - 1)))
                        for s in range(2):
                            h = 2 * pair + s
                            ins = pe.matmul(scoresT[:, u % 2, s, 0:T - first],
                                            heads[0:ROWMAX + 1, 1, h, j * P:(j + 1) * P],
                                            heads[0:ROWMAX + 1, 0, h, first:T], start=True, stop=True)
                        ins.then_inc(st_filled.sem, 1)

                def times_v(i, a, g, j):
                    n = a * NG + g
                    m = TT * n + j
                    if j == 0:
                        pe.wait_ge(*out_done.after(i, n))
                    if g == 0:
                        pe.wait_ge(*banks.out(i, ("v", a, j)))
                    pe.wait_ge(*causal.after(i, m + 1))
                    for to, is_sum in ((out_ps, False), (sum_ps, True)):
                        for h in range(GH):
                            head = (GH * g + h) * HD
                            left = ones[:, :] if is_sum else v[:, j, head:head + HD]
                            ins = pe.matmul(to[h * HD:(h + 1) * HD, P * j:T], left,
                                            probs[:, m % 2, h, 0:T - P * j],
                                            start=(j == 0), stop=(j == TT - 1))
                    ins.then_inc(pv_done.sem, 1)

                def output(i, a, t, last):
                    name = "y", a, t
                    if not last:
                        pe.wait_ge(*banks.empty(i, name))
                        pe.wait_ge(*out_done.after(i, a * NG + NG - 1))
                    else:
                        pe.wait_ge(*out_done.after(i, (a + 1) * NG))
                    for c in ([CT - 1] if last else range(CT - 1)):
                        ins = pe.matmul(banks.bank(name), tile_of(xT, c, t), wo[:, a, c, :],
                                        start=(c == 0), stop=(c == CT - 1))
                    if last:
                        ins.then_inc(filled, 1)

                def attend(i, a):
                    for step, g, h in attention_order(a):
                        if step == "P":
                            project(i, a, g, h)
                        if step == "T":
                            transpose_group(i, a, g)
                        if step == "V":
                            values(i, a, g)
                        if step == "S":
                            scores(i, a, g, h)
                        if step == "M":
                            transpose_max(i, a, g)
                        if step == "ST":
                            scores_less_max(i, a, g, h)
                        if step == "PV":
                            times_v(i, a, g, h)
                        if step == "Y":
                            output(i, a, g, h == 1)

                pe.wait_ge(consts, N_CONSTS)
                pe.wait_ge(qkv_in, 32)
                pe.wait_ge(rest_in, 16 * N_REST)
                with pe.Fori(0, blocks) as i:
                    pe.wait_ge(*first_normed.after(i, TT))
                    for c in range(CT):
                        transpose_columns(i, ("xT", c), x1, c)
                    pe.wait_ge(*banks.out(i, ("xT", CT - 1)))
                    attend(i, 0)
                    pe.wait_ge(*xr_done.after(i, TT))
                    for c in range(CT):
                        transpose_columns(i, ("xrT", c), y, c)
                    pe.wait_ge(*banks.out(i, ("xrT", CT - 1)))
                    for m in range(2):
                        pe.wait_ge(*banks.empty(i, ("lat", m)))
                        product(banks.bank(("lat", m)), [(wlat[:, c, m, :], xT[:, c, :]) for c in range(CT)])\
                            .then_inc(filled, 1)
                    pe.wait_ge(*banks.out(i, ("lat", 1)))
                    attend(i, 1)


def norm_order():
    for t in range(TT + 2):
        if t < TT:
            yield "A", t
        if 1 <= t <= TT:
            yield "B", t - 1
        if t >= 2:
            yield "C", t - 2


def expert_layer(nc, h_in, x1_in, ln2_w, weights, out, blocks):
    sh_gate, sh_up, sh_down, r_gate, r_up, r_down, router_w, router_b = weights
    with ExitStack() as ctx:
        def sb(name, shape, dt=F32):
            return ctx.enter_context(nc.sbuf_tensor(name, shape, dt))

        signals = []

        def signal(name, per_pass):
            signals.append(Signal(ctx.enter_context(nc.semaphore(name)), per_pass))
            return signals[-1]

        wg = sb("wg", [P, NE, CT, FF])
        wu = sb("wu", [P, NE, CT, FF])
        wd = sb("wd", [P, NE, FT, D])
        wr = sb("wr", [P, CT, NR])
        rb = sb("rb", [NR, 1])
        ln2w = sb("ln2w", [P, CT])
        ident = sb("ident2", [P, P])
        number = sb("number", [P, NR])
        h = sb("h", [P, 2, TT, D])
        x1 = sb("x1b", [P, 2, TT, D])
        xr = sb("xr", [P, TT, D])
        xT = sb("xT2", [P, CT, T])
        actT = sb("actT", [P, 2, FT, T])
        tanh = sb("tanh", [P, 2, T])
        gated = sb("gated", [P, 2, T])
        zT = sb("zT", [P, T])
        half = sb("half", [P, TT, NR])
        chance = sb("chance", [P, TT, 8])
        best = sb("best", [P, TT, 8])
        where = sb("where", [P, TT, 8], U32)
        wheref = sb("wheref", [P, TT, 2])
        den = sb("den", [P, TT])
        rden = sb("rden", [P, TT])
        share = sb("share", [P, TT, 2])
        part = sb("part", [P, 2, TT, NR])
        gain = sb("gain", [P, TT, NR])
        unused = sb("unused2", [P, TT, D])
        square = sb("square", [P, TT])
        padded = sb("padded2", [P, 2, TT])
        minus_half = sb("minus_half2", [P, TT])
        rms = sb("rms_h", [P, TT])
        stats = sb("stats2", [P, TT, 6])
        meanvar = sb("meanvar2", [P, TT, 2])
        rstd = sb("rstd2", [P, TT])

        names = loop2_fills()
        ring = ctx.enter_context(nc.psum_tensor("ring2", [P, 7, 512], F32))
        filled = ctx.enter_context(nc.semaphore("ring2_filled"))
        freed = [ctx.enter_context(nc.semaphore(f"ring2_freed{n}")) for n in range(7)]
        banks = Banks(ring, filled, freed, names)

        small_in = ctx.enter_context(nc.semaphore("small_in"))
        expert_in = [ctx.enter_context(nc.semaphore(f"expert_in{e}")) for e in range(NE)]
        consts = ctx.enter_context(nc.semaphore("consts2"))
        consts_step = ctx.enter_context(nc.semaphore("consts2_step"))
        N_CONSTS = 5
        padded_done = signal("padded2_done", 2)
        N_SMALL = 3
        h_loaded = signal("h_loaded", 16)
        x1_loaded = signal("x1_loaded", 16)
        squared = signal("squared", TT)
        rms_done = signal("rms_done", 1)
        xr_done = signal("xr_done2", TT)
        pool_turn = ctx.enter_context(nc.semaphore("pool_turn2"))
        dve_turn = ctx.enter_context(nc.semaphore("dve_turn2"))
        sp_turn = ctx.enter_context(nc.semaphore("sp_turn2"))
        chance_done = signal("chance_done", 1)
        ROUTE = 2 * TT + 4 + 2 * TT + 1
        route_step = signal("route_step", ROUTE)
        tanh_done = signal("tanh_done", NE * FT)
        gated_step = signal("gated_step", 0)
        stats_done = signal("stats2_done", TT)
        meanvar_done = signal("meanvar2_done", TT)
        rstd_done = signal("rstd2_done", 1)
        closed = signal("closed", TT)
        out_ready = signal("out_ready", TT)
        stored = signal("stored", 16)

        with nc.Block() as block:
            @block.sync
            def _(sp):
                for s in signals:
                    sp.sem_inc(s.sem, 1)
                for sem in [filled, *freed]:
                    sp.sem_inc(sem, 1)

        with nc.Block() as block:
            @block.sync
            def _(sp):
                sp.dma_start(ln2w[:, :], ln2_w).then_inc(small_in, 16)
                sp.dma_start(wr[:, :, :], router_w.rearrange("(c p) n -> p c n", p=P)).then_inc(small_in, 16)
                sp.dma_start(rb[:, :], router_b).then_inc(small_in, 16)
                with sp.Fori(0, blocks) as i:
                    sp.wait_ge(*stored.after(i, 0))
                    sp.sem_inc(sp_turn, 1)
                    rows = "o (t p) c -> p (o t) c"
                    sp.dma_start(h[:, 0], h_in[bass.ds(i, 1), :, :].rearrange(rows, p=P)).then_inc(h_loaded.sem, 16)
                    sp.dma_start(x1[:, 0], x1_in[bass.ds(i, 1), :, :].rearrange(rows, p=P)).then_inc(x1_loaded.sem, 16)
                    sp.wait_ge(*out_ready.after(i, TT))
                    sp.sem_inc(sp_turn, 1)
                    sp.dma_start(out[bass.ds(i, 1), :, :].rearrange(rows, p=P), x1[:, 0]).then_inc(stored.sem, 16)
                sp.wait_ge(*stored.after(blocks - 1, 16))

            @block.gpsimd
            def _(pool):
                pool.memset(ident[:, :], 0.0).then_inc(consts_step, 1)
                pool.memset(zT[:, :], 0.0).then_inc(consts, 1)
                pool.memset(minus_half[:, :], -0.5).then_inc(consts, 1)
                pool.memset(chance[:, :, :], -1.0).then_inc(consts, 1)
                pool.iota(number[:, :], pattern=[[1, NR]], base=0, channel_multiplier=0,
                          allow_small_or_imprecise_dtypes=True).then_inc(consts, 1)
                pool.wait_ge(consts_step, 1)
                pool.affine_select(out=ident[:, :], in_=ident[:, :], compare_op=ALU.not_equal, fill=1.0,
                                   base=0, pattern=[[-1, P]], channel_multiplier=1).then_inc(consts, 1)
                with pool.Fori(0, blocks) as i:
                    pool.wait_ge(*squared.after(i, TT))
                    pool.sem_inc(pool_turn, 1)
                    pool.tensor_scalar(padded[:, 0, :], square[:, :], EPS, None, ALU.add).then_inc(padded_done.sem, 1)
                    pool.wait_ge(*padded_done.after(i, 1))
                    pool.tensor_tensor(rms[:, :], padded[:, 0, :], minus_half[:, :], ALU.pow)\
                        .then_inc(rms_done.sem, 1)
                    pool.wait_ge(*meanvar_done.after(i, TT))
                    pool.sem_inc(pool_turn, 1)
                    pool.tensor_scalar(padded[:, 1, :], meanvar[:, :, 1], EPS, None, ALU.add).then_inc(padded_done.sem, 1)
                    pool.wait_ge(*padded_done.after(i, 2))
                    pool.tensor_tensor(rstd[:, :], padded[:, 1, :], minus_half[:, :], ALU.pow)\
                        .then_inc(rstd_done.sem, 1)

            @block.scalar
            def _(act):
                for e in range(NE):
                    gate, up, down = (sh_gate, sh_up, sh_down) if e == 0 else (r_gate[e - 1], r_up[e - 1], r_down[e - 1])
                    for to, of in ((wg, gate), (wu, up), (wd, down)):
                        act.dma_start(to[:, e], of.rearrange("(c p) n -> p c n", p=P)).then_inc(expert_in[e], 16)
                act.wait_ge(consts, N_CONSTS)
                act.wait_ge(small_in, 16 * N_SMALL)
                with act.Fori(0, blocks) as i:
                    for c in range(CT):
                        act.wait_ge(*banks.full(i, ("xT", c)))
                        act.activation(xT[:, c, :], banks.bank(("xT", c)), ACT.Copy, scale=ln2w[:, c:c + 1])\
                           .then_inc(banks.release(("xT", c)), 1)
                    act.wait_ge(*banks.full(i, ("z", 0)))
                    act.activation(zT[0:NR, :], banks.bank(("z", 0))[0:NR, :], ACT.Identity, bias=rb[:, 0:1])\
                       .then_inc(banks.release(("z", 0)), 1)
                    act.wait_ge(*banks.full(i, ("zT", 0)))
                    act.activation(half[:, :, :],
                                   banks.bank(("zT", 0)).rearrange("p (t n) -> p t n", t=TT)[:, :, 0:NR],
                                   ACT.Tanh, scale=0.5).then_inc(banks.release(("zT", 0)), 1)
                    for step in expert_order():
                        if step[0] == "GU":
                            _, e, m = step
                            n = e * FT + m
                            if n >= 2:
                                act.wait_ge(*banks.out(i, ("gate", *divmod(n - 2, FT))))
                            act.wait_ge(*banks.full(i, ("gate", e, m)))
                            act.activation(tanh[:, n % 2, :], banks.bank(("gate", e, m)), ACT.Tanh, scale=0.5)\
                               .then_inc(tanh_done.sem, 1)

            @block.vector
            def _(dve):
                dve.wait_ge(consts, N_CONSTS)

                def routing(i):
                    steps = [0]

                    def step(ins):
                        steps[0] += 1
                        ins.then_inc(route_step.sem, 1)

                    def so_far():
                        dve.wait_ge(*route_step.after(i, steps[0]))
                        dve.sem_inc(dve_turn, 1)

                    dve.wait_ge(*banks.out(i, ("zT", 0)))
                    dve.tensor_scalar(chance[:, :, 0:NR], half[:, :, :], 0.5, 0.5, ALU.mult, ALU.add)\
                       .then_inc(chance_done.sem, 1)
                    dve.wait_ge(*chance_done.after(i, 1))
                    dve.sem_inc(dve_turn, 1)
                    for t in range(TT):
                        step(dve.max(best[:, t, :], chance[:, t, :]))
                    so_far()
                    for t in range(TT):
                        step(dve.max_index(where[:, t, :], best[:, t, :], chance[:, t, :]))
                    step(dve.tensor_tensor(den[:, :], best[:, :, 0], best[:, :, 1], ALU.add))
                    so_far()
                    step(dve.reciprocal(rden[:, :], den[:, :]))
                    step(dve.tensor_copy(wheref[:, :, :], where[:, :, 0:2]))
                    so_far()
                    step(dve.tensor_tensor(share[:, :, :], best[:, :, 0:2],
                                           rden[:, :].unsqueeze(2).to_broadcast([P, TT, 2]), ALU.mult))
                    so_far()
                    for s in range(2):
                        for t in range(TT):
                            step(dve.tensor_scalar(part[:, s, t, :], number[:, :], wheref[:, t, s:s + 1],
                                                   share[:, t, s:s + 1], ALU.is_equal, ALU.mult))
                    so_far()
                    step(dve.tensor_tensor(gain[:, :, :], part[:, 0], part[:, 1], ALU.add))
                    so_far()
                    assert steps[0] == ROUTE

                def activate(i, e, m):
                    n = e * FT + m
                    dve.wait_ge(*tanh_done.after(i, n + 1))
                    dve.scalar_tensor_tensor(out=gated[:, n % 2, :], in0=tanh[:, n % 2, :], scalar=1.0,
                                             in1=banks.bank(("gate", e, m)), op0=ALU.add, op1=ALU.mult)\
                       .then_inc(banks.release(("gate", e, m)), 1)
                    dve.wait_ge(*banks.out(i, ("gate", e, m)))
                    dve.wait_ge(*banks.full(i, ("up", e, m)))
                    dve.scalar_tensor_tensor(out=actT[:, e % 2, m, :], in0=gated[:, n % 2, :], scalar=1.0 / 16.0,
                                             in1=banks.bank(("up", e, m)), op0=ALU.mult, op1=ALU.mult)\
                       .then_inc(banks.release(("up", e, m)), 1)

                def add_expert(i, e):
                    for t in range(TT):
                        name = ("down", e, t)
                        dve.wait_ge(*banks.full(i, name))
                        if e == 0:
                            ins = dve.tensor_tensor(h[:, 0, t, :], banks.bank(name), h[:, 0, t, :], ALU.add)
                        else:
                            dve.wait_ge(*banks.out(i, ("down", e - 1, t)))
                            ins = dve.scalar_tensor_tensor(out=h[:, 0, t, :], in0=banks.bank(name),
                                                           scalar=gain[:, t, e - 1:e], in1=h[:, 0, t, :],
                                                           op0=ALU.mult, op1=ALU.add)
                        ins.then_inc(banks.release(name), 1)

                with dve.Fori(0, blocks) as i:
                    dve.wait_ge(*h_loaded.after(i, 16))
                    for t in range(TT):
                        dve.tensor_tensor_reduce(unused[:, t, :], h[:, 0, t, :], h[:, 0, t, :], 1.0 / D, 0.0,
                                                 ALU.mult, ALU.add, square[:, t:t + 1]).then_inc(squared.sem, 1)
                    dve.wait_ge(*rms_done.after(i, 1))
                    for t in range(TT):
                        dve.tensor_scalar(xr[:, t, :], h[:, 0, t, :], rms[:, t:t + 1], None, ALU.mult)\
                           .then_inc(xr_done.sem, 1)
                    routing(i)
                    for step in expert_order():
                        if step[0] == "GU":
                            activate(i, *step[1:])
                        else:
                            add_expert(i, step[1])
                    for t in range(TT):
                        dve.wait_ge(*banks.out(i, ("down", NE - 1, t)))
                        dve.bn_stats(stats[:, t, :], h[:, 0, t, :]).then_inc(stats_done.sem, 1)
                    for t in range(TT):
                        dve.wait_ge(*stats_done.after(i, t + 1))
                        dve.sem_inc(dve_turn, 1)
                        dve.bn_aggr(meanvar[:, t, :], stats[:, t, :]).then_inc(meanvar_done.sem, 1)
                    dve.wait_ge(*rstd_done.after(i, 1))
                    for t in range(TT):
                        dve.tensor_scalar(xr[:, t, :], h[:, 0, t, :], meanvar[:, t, 0:1], rstd[:, t:t + 1],
                                          ALU.subtract, ALU.mult).then_inc(closed.sem, 1)
                    dve.wait_ge(*x1_loaded.after(i, 16))
                    for t in range(TT):
                        dve.wait_ge(*closed.after(i, t + 1))
                        dve.tensor_tensor(x1[:, 0, t, :], xr[:, t, :], x1[:, 0, t, :], ALU.add)\
                           .then_inc(out_ready.sem, 1)

            @block.tensor
            def _(pe):
                pe.wait_ge(consts, N_CONSTS)
                pe.wait_ge(small_in, 16 * N_SMALL)
                def product(to, pairs):
                    for n, (left, right) in enumerate(pairs):
                        ins = pe.matmul(to, left, right, start=(n == 0), stop=(n == len(pairs) - 1))
                    return ins

                with pe.Fori(0, blocks) as i:
                    pe.wait_ge(*xr_done.after(i, TT))
                    for c in range(CT):
                        to = banks.bank(("xT", c))
                        pe.wait_ge(*banks.empty(i, ("xT", c)))
                        for t in range(TT):
                            ins = pe.transpose(to[:, t * P:(t + 1) * P], xr[:, t, c * P:(c + 1) * P], ident[:, :])
                        ins.then_inc(filled, 1)
                    to = banks.bank(("z", 0))
                    pe.wait_ge(*banks.empty(i, ("z", 0)))
                    for c in range(CT):
                        pe.wait_ge(*banks.out(i, ("xT", c)))
                    product(to[0:NR, :], [(wr[:, c, :], xT[:, c, :]) for c in range(CT)]).then_inc(filled, 1)
                    to = banks.bank(("zT", 0))
                    pe.wait_ge(*banks.empty(i, ("zT", 0)))
                    pe.wait_ge(*banks.out(i, ("z", 0)))
                    for t in range(TT):
                        ins = pe.transpose(to[:, t * P:(t + 1) * P], zT[:, t * P:(t + 1) * P], ident[:, :])
                    ins.then_inc(filled, 1)
                    for step in expert_order():
                        if step[0] == "GU":
                            _, e, m = step
                            pe.wait_ge(expert_in[e], 48)
                            for name, w in (("gate", wg), ("up", wu)):
                                to = banks.bank((name, e, m))
                                pe.wait_ge(*banks.empty(i, (name, e, m)))
                                product(to, [(w[:, e, c, m * P:(m + 1) * P], xT[:, c, :]) for c in range(CT)])\
                                    .then_inc(filled, 1)
                        else:
                            e = step[1]
                            for m in range(FT):
                                pe.wait_ge(*banks.out(i, ("up", e, m)))
                            for t in range(TT):
                                to = banks.bank(("down", e, t))
                                pe.wait_ge(*banks.empty(i, ("down", e, t)))
                                product(to, [(actT[:, e % 2, m, t * P:(t + 1) * P], wd[:, e, m, :])
                                             for m in range(FT)]).then_inc(filled, 1)


def build(nc, a, out, blocks):
    kept = [nc.dram_tensor(name, (blocks, T, D), F32, kind="Internal").ap() for name in ("x1_kept", "h_kept")]
    attention_layers(nc, a["L0_attn_x"],
                     [a[n] for n in ("L0_attn_w_qkv", "L0_attn_w_o")] +
                     [a[f"L0_ffn_{n}"] for n in ("kv_d_w", "q_d_w", "k_u_w", "v_u_w", "q_u_w", "rope_k_w",
                                                 "rope_q_w", "o_w")],
                     (a["rope1"], a["rope2"]), a["L0_ffn_ln1_w"], kept[0], kept[1], blocks)
    expert_layer(nc, kept[1], kept[0], a["L0_ffn_ln2_w"],
                 [a[f"L0_ffn_{n}"] for n in ("sh_gate", "sh_up", "sh_down", "r_gate", "r_up", "r_down",
                                             "router_w", "router_b")], out, blocks)


def rope_table(width):
    inverse = (np.float32(1.0) / np.float32(10000.0) ** (np.arange(0, width, 2, dtype=np.float32) / np.float32(width)))
    angle = np.outer(np.arange(T, dtype=np.float32), inverse.astype(np.float32)).astype(np.float32)
    cos, sin = np.cos(angle), np.sin(angle)
    table = np.stack([np.concatenate([cos, cos], 1), np.concatenate([-sin, sin], 1)], 1)
    return np.ascontiguousarray(table.reshape(TT, P, 2, width).transpose(1, 0, 2, 3).astype(np.float32))


def kernel(**inputs):
    import concourse.bacc as bacc
    from concourse.bass_utils import run_bass_kernel_spmd

    nc = bacc.Bacc("TRN2", target_bir_lowering=False, num_devices=1)
    arrays, a = {}, {}
    tables = {"rope1": rope_table(HD), "rope2": rope_table(RD)}
    for name, value in {**inputs, **tables}.items():
        if name in ("L0_ffn_ln1_w", "L0_ffn_ln2_w"):
            value = np.asarray(value).reshape(CT, P).T
        if name == "L0_ffn_router_b":
            value = np.asarray(value).reshape(NR, 1)
        value = np.ascontiguousarray(value)
        arrays[f"in_{name}"] = value
        a[name] = nc.dram_tensor(f"in_{name}", value.shape, mybir.dt.from_np(value.dtype), kind="ExternalInput").ap()
    blocks = inputs["L0_attn_x"].shape[0]
    out = nc.dram_tensor("out", (blocks, T, D), F32, kind="ExternalOutput").ap()
    build(nc, a, out, blocks)
    result = run_bass_kernel_spmd(nc, [arrays], core_ids=[0])
    return result.results[0]["out"]
```

```python
from contextlib import ExitStack

import numpy as np

import concourse.bass as bass
from concourse import mybir

F32 = mybir.dt.float32
F32R = mybir.dt.float32r
BF16 = mybir.dt.bfloat16
U32 = mybir.dt.uint32
ALU = mybir.AluOpType
ACT = mybir.ActivationFunctionType

P = 128
D = 512
CT = D // P
T = 512
TT = T // P
NH = 16
HD = D // NH
GH = P // HD
NG = NH // GH
RD = HD // 2
LAT = D // 4
FF = 256
FT = FF // P
NR = 7
NE = NR + 1
EPS = 1e-5
SCALE = float(HD) ** -0.5
MASKED = -3.0e38
ROWMAX = 3 * HD
STACKS = 3
NB = 4
PAIRS = NE // 2
WIDE = CT * FF
CHUNKS = 3 * WIDE // 512
CHUNKS_IN = {0: (0, 1), 1: (2, 3), 2: (4, 5)}


class Signal:

    def __init__(self, sem, per_pass, start=1):
        self.sem, self.per_pass, self.start = sem, per_pass, start

    def after(self, i, k):
        return self.sem, i * self.per_pass + (k + self.start)


class Banks:

    def __init__(self, tensor, filled, freed, names):
        self.tensor, self.filled, self.freed = tensor, filled, freed
        self.n = len(freed)
        assert len(names) % self.n == 0 and len(set(names)) == len(names)
        self.number = {name: k for k, name in enumerate(names)}
        self.per_pass = len(names)

    def at(self, name):
        return self.number[name] % self.n

    def bank(self, name):
        return self.tensor[:, self.at(name), :]

    def full(self, i, name):
        return self.filled, i * self.per_pass + (self.number[name] + 2)

    def empty(self, i, name):
        return self.freed[self.at(name)], i * (self.per_pass // self.n) + (self.number[name] // self.n + 1)

    def out(self, i, name):
        return self.freed[self.at(name)], i * (self.per_pass // self.n) + (self.number[name] // self.n + 2)

    def release(self, name):
        return self.freed[self.at(name)]


def attention_order(a):
    if a == 0:
        yield from [("P", 0, 0), ("P", 0, 1), ("P", 1, 0), ("T", 0), ("P", 1, 1), ("V", 0), ("V", 1),
                    ("T", 1), ("V", 2), ("S", 0, 0), ("V", 3), ("S", 0, 1), ("S", 0, 2), ("P", 2, 0), ("S", 0, 3),
                    ("P", 2, 1), ("M", 0), ("P", 3, 0), ("T", 2)]
    else:
        yield from [("P", 0, 0), ("P", 0, 1), ("P", 1, 0), ("P", 1, 1), ("T", 0), ("V", 0), ("V", 1),
                    ("V", 2), ("V", 3), ("P", 2, 0), ("P", 2, 1), ("T", 1), ("S", 0, 0), ("S", 0, 1),
                    ("S", 0, 2), ("S", 0, 3), ("P", 3, 0), ("M", 0), ("T", 2), ("P", 3, 1)]

    def transposed_scores(g, j, pair):
        return [("ST", g, j, 2 * pair), ("ST", g, j, 2 * pair + 1)]

    for g in range(NG - 1):
        closing = [("C", g - 1, t) for t in range(TT)] if g else []
        yield from transposed_scores(g, 0, 0)
        yield from transposed_scores(g, 0, 1)
        if g:
            yield "O", g - 1
        yield "S", g + 1, 0
        if g == 1:
            yield "T", 3
        yield from transposed_scores(g, 1, 0)
        yield "S", g + 1, 1
        yield from transposed_scores(g, 1, 1)
        yield "S", g + 1, 2
        yield "PV", g, 0
        yield "S", g + 1, 3
        yield from transposed_scores(g, 2, 0)
        yield from transposed_scores(g, 2, 1)
        yield "M", g + 1
        yield from closing[0:4]
        if a == 1 and g == NG - 2:
            yield from [("L", t) for t in range(TT)]
        yield "PV", g, 1
        if a == 0 and g == 0:
            yield "P", 3, 1
        yield from transposed_scores(g, 3, 0)
        yield from transposed_scores(g, 3, 1)
        yield from [("PV", g, 2), ("PV", g, 3)]
    g = NG - 1
    yield from transposed_scores(g, 0, 0)
    yield from transposed_scores(g, 0, 1)
    yield "O", g - 1
    yield from [("C", g - 1, t) for t in range(TT)]
    if a == 1:
        yield ("R",)
    for pair in range(2):
        yield from transposed_scores(g, 1, pair)
    yield "PV", g, 0
    for pair in range(2):
        yield from transposed_scores(g, 2, pair)
    if a == 1:
        yield from [("N", t) for t in range(TT)]
    yield "PV", g, 1
    for pair in range(2):
        yield from transposed_scores(g, 3, pair)
    yield "Y", 0, 0
    yield from [("PV", g, 2), ("PV", g, 3), ("O", g), ("Y", 1, 0), ("Y", 2, 0), *(("C", g, t) for t in range(TT)),
                ("Y", 0, 1), ("Y", 1, 1), ("Y", 2, 1), ("Y", 3, 0), ("Y", 3, 1)]


def attention_fills(a):
    for step, *which in attention_order(a):
        if step == "P":
            g, keys = which
            yield ("q", "k")[keys], a, g
        if step == "T":
            yield from [("qT", a, *which), ("kT", a, *which)]
        if step == "V":
            yield "v", a, *which
        if step == "S":
            yield from [("S", a, *which, part) for part in range(3)]
        if step == "M":
            yield "M", a, *which
        if step == "Y" and which[1] == 0:
            yield "y", a, which[0]


def loop1_fills():
    names = [("xT", c) for c in range(CT)]
    names += attention_fills(0)
    names += [("xrT", c) for c in range(CT)]
    names += [("lat", m) for m in range(2)]
    names += attention_fills(1)
    return names

def attention_layers(nc, x, weights, tables, ln1_w, x1_out, h_out, blocks):
    w_qkv, w_o, kv_d, q_d, k_u, v_u, q_u, rope_k, rope_q, o_w = weights
    with ExitStack() as ctx:
        signals = []

        def sb(name, shape, dt=F32):
            return ctx.enter_context(nc.sbuf_tensor(name, shape, dt))

        def semaphore(name):
            return ctx.enter_context(nc.semaphore(name))

        def signal(name, per_pass):
            signals.append(Signal(semaphore(name), per_pass))
            return signals[-1]

        wqkv = sb("wqkv", [P, CT, 3 * D])
        wo = sb("wo", [P, 2, CT, D])
        wlat = sb("wlat", [P, CT, 2, LAT])
        wku = sb("wku", [P, NH * RD])
        wvu = sb("wvu", [P, D])
        wq2 = sb("wq2", [P, NH, 2, RD])
        wkr = sb("wkr", [P, CT, NH * RD])
        rope1 = sb("rope1", [P, TT, 2, HD])
        rope2 = sb("rope2", [P, TT, 2, RD])
        ln1w = sb("ln1w", [P, CT])
        ident = sb("ident", [P, P])
        ones = sb("ones", [P, HD])
        minus_half = sb("minus_half", [P, TT])
        mask = sb("mask", [P, T])

        x_in = sb("x_in", [P, TT, D])
        x1 = sb("x1", [P, TT, D])
        xin = sb("xin", [P, TT, D])
        outT = sb("outT", [P, NG, T])
        xT = sb("xT", [P, CT, T])
        v = sb("v", [P, TT, D])
        latT = sb("latT", [P, 2, T])
        qk = sb("qk", [P, 2, 2, TT, P])
        turned = sb("turned", [P, 2, 2, T])
        parts = sb("parts", [P, 4, T], F32R)
        stacks = [sb(f"stacks{n}", [P, 2, GH, T], F32R) for n in range(STACKS)]
        probs = sb("probs", [P, 2, GH, T])
        total = sb("total", [P, T])
        whole = sb("whole", [P, T])
        unused = sb("unused", [P, TT, T], BF16)
        rowmax = sb("rowmax", [P, 2, GH * TT])
        negmax = sb("negmax", [GH * TT, 2, P], F32R)
        stats = sb("stats", [P, 3, TT, 6])
        meanvar = sb("meanvar", [P, 3, TT, 2])
        padded = sb("padded", [P, 3, TT, 2])
        rstd = sb("rstd", [P, 3, TT, 2])
        minus_mean = sb("minus_mean", [P, 2, TT, 1])
        shift = sb("shift", [P, 2, TT, 2])

        ring = ctx.enter_context(nc.psum_tensor("ring", [P, 3, 512], F32))
        scoresT = ctx.enter_context(nc.psum_tensor("scoresT", [P, 3, 512], F32))
        out_ps = ctx.enter_context(nc.psum_tensor("out_ps", [P, 512], F32))
        sum_ps = ctx.enter_context(nc.psum_tensor("sum_ps", [P, 512], F32))

        names = loop1_fills()
        filled = semaphore("ring_filled")
        freed = [semaphore(f"ring_freed{n}") for n in range(3)]
        banks = Banks(ring, filled, freed, names)

        qkv_in = semaphore("qkv_in")
        rest_in = semaphore("rest_in")
        N_REST = 11
        consts = semaphore("consts")
        consts_step = semaphore("consts_step")
        N_CONSTS = 4 + STACKS
        pool_turn, dve_turn, sp_turn, act_turn = (semaphore(f"{e}_turn") for e in ("pool", "dve", "sp", "act"))
        x_loaded = signal("x_loaded", 16)
        first_normed = signal("first_normed", TT)
        stats_done = [signal(f"stats_done{n}", TT) for n in range(3)]
        meanvar_done = [signal(f"meanvar_done{n}", TT) for n in range(3)]
        padded_done = [signal(f"padded_done{n}", (1, 2 * TT, 3 * TT)[n]) for n in range(3)]
        shift_done = [signal(f"shift_done{n}", TT) for n in range(2)]
        rstd_done = [signal(f"rstd_done{n}", TT if n else 1) for n in range(3)]
        x1_done = signal("x1_done", TT)
        xin_done = signal("xin_done", TT)
        xr_done = signal("xr_done", TT)
        x1_stored = signal("x1_stored", 16)
        h_stored = signal("h_stored", 16)
        cos_done = signal("cos_done", 4 * NG)
        rotated = signal("rotated", 4 * NG)
        plain_done = signal("plain_done", 2 * NG)
        high_done = signal("high_done", 2 * 2 * NG)
        PER_STACK = 3 * 16
        stacked = [[signal(f"stacked{n}_{h}", PER_STACK) for h in range(GH)] for n in range(2 * NG)]
        negmax_in = [signal(f"negmax_in{n}", NG * 16) for n in range(2)]
        max_done = signal("max_done", 2 * NH)
        st_filled = signal("st_filled", 2 * NG * TT * GH)
        exp_done = signal("exp_done", 2 * NG * TT * GH)
        causal = signal("causal", 2 * NG * TT)
        pv_done = signal("pv_done", 2 * NG * TT)
        taken = signal("taken", 2 * NG)
        total_done = signal("total_done", 2 * NG * TT)
        out_done = signal("out_done", 2 * NG * TT)

        with nc.Block() as block:
            @block.sync
            def _(sp):
                for s in signals:
                    sp.sem_inc(s.sem, 1)
                for sem in [filled, *freed]:
                    sp.sem_inc(sem, 1)

        with nc.Block() as block:

            @block.sync
            def _(sp):
                in_rows = "o (t p) c -> p (o t) c"
                by_c = "(c p) n -> p c n"
                sp.dma_start(x_in[:, :, :], x[0:1, :, :].rearrange(in_rows, p=P)).then_inc(x_loaded.sem, 16)
                sp.dma_start(rope1[:, :, :, :], tables[0]).then_inc(qkv_in, 16)
                sp.dma_start(wqkv[:, :, :], w_qkv.rearrange(by_c, p=P)).then_inc(qkv_in, 16)
                sp.dma_start(wo[:, 0], w_o.rearrange(by_c, p=P)).then_inc(rest_in, 16)
                sp.dma_start(rope2[:, :, :, :], tables[1]).then_inc(rest_in, 16)
                sp.dma_start(ln1w[:, :], ln1_w).then_inc(rest_in, 16)
                sp.dma_start(wlat[:, :, 0, :], kv_d.rearrange(by_c, p=P)).then_inc(rest_in, 16)
                sp.dma_start(wlat[:, :, 1, :], q_d.rearrange(by_c, p=P)).then_inc(rest_in, 16)
                sp.dma_start(wku[:, :], k_u).then_inc(rest_in, 16)
                sp.dma_start(wvu[:, :], v_u).then_inc(rest_in, 16)
                sp.dma_start(wq2[:, :, 0, :], q_u.rearrange("p (h d) -> p h d", h=NH)).then_inc(rest_in, 16)
                sp.dma_start(wq2[:, :, 1, :], rope_q.rearrange("p (h d) -> p h d", h=NH)).then_inc(rest_in, 16)
                sp.dma_start(wkr[:, :, :], rope_k.rearrange(by_c, p=P)).then_inc(rest_in, 16)
                sp.dma_start(wo[:, 1], o_w.rearrange(by_c, p=P)).then_inc(rest_in, 16)
                sp.wait_ge(consts, N_CONSTS)

                def stack(i, a, g):
                    n = a * NG + g
                    sp.wait_ge(*high_done.after(i, 2 * (n + 1)))
                    sp.sem_inc(sp_turn, 1)
                    sp.wait_ge(*banks.out(i, ("qT", a, g)))
                    sp.sem_inc(sp_turn, 1)
                    sp.wait_ge(*banks.out(i, ("kT", a, g)))
                    sp.sem_inc(sp_turn, 1)
                    sp.wait_ge(*st_filled.after(i, max(0, GH * TT * (n - STACKS + 1))))
                    sp.sem_inc(sp_turn, 1)
                    for h in range(GH):
                        for s, chosen in enumerate((slice(0, 2), slice(2, 0, -1), slice(0, 4, 3))):
                            sp.dma_start(stacks[n % STACKS][s * HD:(s + 1) * HD, :, h, :].bitcast(F32),
                                         parts[h * HD:(h + 1) * HD, chosen, :].bitcast(F32))\
                              .then_inc(stacked[n][h].sem, 16)

                with sp.Fori(0, blocks) as i:
                    for g in range(NG):
                        stack(i, 0, g)
                    sp.wait_ge(*x1_done.after(i, TT))
                    sp.sem_inc(sp_turn, 1)
                    sp.dma_start(x1_out[bass.ds(i, 1), :, :].rearrange(in_rows, p=P), x1[:, :, :])\
                      .then_inc(x1_stored.sem, 16)
                    sp.dma_start(x_in[:, :, :], x[bass.ds((i + 1) % blocks, 1), :, :].rearrange(in_rows, p=P))\
                      .then_inc(x_loaded.sem, 16)
                    for g in range(NG):
                        stack(i, 1, g)
                    for t in range(1, TT):
                        sp.wait_ge(*banks.out(i, ("y", 1, t)))
                        sp.sem_inc(sp_turn, 1)
                    sp.dma_start(h_out[bass.ds(i, 1), :, :].rearrange(in_rows, p=P), v[:, :, :])\
                      .then_inc(h_stored.sem, 16)
                sp.wait_ge(*x1_stored.after(blocks - 1, 16))
                sp.wait_ge(*h_stored.after(blocks - 1, 16))
                sp.wait_ge(*x_loaded.after(blocks - 1, 32))

            @block.gpsimd
            def _(pool):
                pool.memset(ones[:, :], 1.0).then_inc(consts, 1)
                pool.memset(minus_half[:, :], -0.5).then_inc(consts, 1)
                pool.memset(ident[:, :], 0.0).then_inc(consts_step, 1)
                pool.memset(mask[:, :], 0.0).then_inc(consts_step, 1)
                pool.wait_ge(consts_step, 2)
                pool.affine_select(out=ident[:, :], in_=ident[:, :], compare_op=ALU.not_equal, fill=1.0,
                                   base=0, pattern=[[-1, P]], channel_multiplier=1).then_inc(consts, 1)
                pool.affine_select(out=mask[:, :], in_=mask[:, :], compare_op=ALU.is_ge, fill=MASKED,
                                   base=T - P, pattern=[[-1, T]], channel_multiplier=1).then_inc(consts, 1)

                def first_roots(i, before):
                    pool.wait_ge(*meanvar_done[0].after(i, before + TT))
                    pool.sem_inc(pool_turn, 1)
                    pool.tensor_scalar(padded[:, 0, :, 0], meanvar[:, 0, :, 1], EPS, None, ALU.add)\
                        .then_inc(padded_done[0].sem, 1)
                    pool.wait_ge(*padded_done[0].after(i, before // TT + 1))
                    pool.tensor_tensor(rstd[:, 0, :, 0], padded[:, 0, :, 0], minus_half[:, 0:TT], ALU.pow)\
                        .then_inc(rstd_done[0].sem, 1)

                def y_root(i, t):
                    pool.wait_ge(*meanvar_done[1].after(i, t + 1))
                    pool.sem_inc(pool_turn, 1)
                    pool.tensor_scalar(padded[:, 1, t, 0:1], meanvar[:, 1, t, 1:2], EPS, None, ALU.add)\
                        .then_inc(padded_done[1].sem, 1)
                    pool.tensor_scalar(minus_mean[:, 0, t, :], meanvar[:, 1, t, 0:1], -1.0, None, ALU.mult)\
                        .then_inc(padded_done[1].sem, 1)
                    pool.wait_ge(*padded_done[1].after(i, 2 * (t + 1)))
                    pool.tensor_tensor(rstd[:, 1, t, 0:1], padded[:, 1, t, 0:1], minus_half[:, 0:1], ALU.pow)\
                        .then_inc(rstd_done[1].sem, 1)
                    pool.wait_ge(*rstd_done[1].after(i, t + 1))
                    pool.tensor_tensor(shift[:, 0, t, 0:1], minus_mean[:, 0, t, :], rstd[:, 1, t, 0:1], ALU.mult)\
                        .then_inc(shift_done[0].sem, 1)

                def x1_roots(i, t):
                    pool.wait_ge(*meanvar_done[2].after(i, t + 1))
                    pool.sem_inc(pool_turn, 1)
                    pool.tensor_scalar(padded[:, 2, t, 0:1], meanvar[:, 2, t, 1:2], EPS, None, ALU.add)\
                        .then_inc(padded_done[2].sem, 1)
                    pool.tensor_scalar(padded[:, 2, t, 1:2], meanvar[:, 2, t, 1:2], 1.0 + EPS, EPS * EPS,
                                       ALU.mult, ALU.add).then_inc(padded_done[2].sem, 1)
                    pool.tensor_scalar(minus_mean[:, 1, t, :], meanvar[:, 2, t, 0:1], -1.0, None, ALU.mult)\
                        .then_inc(padded_done[2].sem, 1)
                    pool.wait_ge(*padded_done[2].after(i, 3 * (t + 1)))
                    pool.tensor_tensor(rstd[:, 2, t, :], padded[:, 2, t, :], minus_half[:, 0:2], ALU.pow)\
                        .then_inc(rstd_done[2].sem, 1)
                    pool.wait_ge(*rstd_done[2].after(i, t + 1))
                    pool.tensor_tensor(shift[:, 1, t, :], minus_mean[:, 1, t, :].to_broadcast([P, 2]),
                                       rstd[:, 2, t, :], ALU.mult).then_inc(shift_done[1].sem, 1)

                def add_rotated(i, a, g, which):
                    r = 2 * (a * NG + g) + which
                    pool.wait_ge(*cos_done.after(i, r + 1))
                    pool.wait_ge(*banks.out(i, (("q", "k")[which], a, g)))
                    if g >= 2:
                        pool.sem_inc(pool_turn, 1)
                        pool.wait_ge(*banks.full(i, ("kT", a, g - 2)))
                    if a == 0:
                        pool.tensor_tensor(qk[:, g % 2, which, :, :].rearrange("p t d -> p (t d)"),
                                           turned[:, r % 2, 0, :], turned[:, r % 2, 1, :], ALU.add)\
                            .then_inc(rotated.sem, 1)
                    else:
                        rows = qk[:, g % 2, which, :, :].rearrange("p t (h s d) -> p (t h) s d", h=GH, s=2)
                        cos_part, sin_part = (turned[:, r % 2, s, 0:T // 2].rearrange("p (t d) -> p t d", d=RD)
                                              for s in range(2))
                        pool.tensor_tensor(rows[:, :, 1, :], cos_part, sin_part, ALU.add).then_inc(rotated.sem, 1)

                def cut(i, n):
                    pool.wait_ge(*exp_done.after(i, GH * (n + 1)))
                    pool.sem_inc(pool_turn, 1)
                    diagonal = probs[:, n % 2, :, 0:P]
                    pool.affine_select(out=diagonal, in_=diagonal, compare_op=ALU.is_ge, fill=0.0,
                                       base=0, pattern=[[0, GH], [1, P]], channel_multiplier=-1)\
                        .then_inc(causal.sem, 1)

                def attend(i, a):
                    for step, *which in attention_order(a):
                        if step == "P":
                            add_rotated(i, a, *which)
                        if step == "ST" and which[2] == GH - 1:
                            cut(i, (a * NG + which[0]) * TT + which[1])
                        if step == "R":
                            first_roots(i, TT)
                        if step == "Y" and which[1] == 1 and a == 0:
                            for kind, t in norm_order(which[0]):
                                if kind == "A":
                                    y_root(i, t)
                                if kind == "B":
                                    x1_roots(i, t)

                pool.wait_ge(consts, N_CONSTS)
                first_roots(0, 0)
                with pool.Fori(0, blocks) as i:
                    attend(i, 0)
                    attend(i, 1)

            @block.scalar
            def _(act):

                def copy(i, name, to, scale=1.0):
                    act.wait_ge(*banks.full(i, name))
                    act.activation(to, banks.bank(name), ACT.Copy, scale=scale)\
                       .then_inc(banks.release(name), 1)

                def take_high(i, a, g):
                    n = a * NG + g
                    for h in range(GH):
                        if n > 0:
                            act.wait_ge(*stacked[n - 1][h].after(i, PER_STACK))
                        else:
                            act.wait_ge(*stacked[2 * NG - 1][h].after(i, 0))
                    for which, name in enumerate(("qT", "kT")):
                        act.wait_ge(*banks.full(i, (name, a, g)))
                        act.activation(parts[:, which, :], banks.bank((name, a, g)), ACT.Copy)\
                           .then_inc(high_done.sem, 1)

                def take_negmax(i, a, g):
                    n = a * NG + g
                    act.wait_ge(*negmax_in[n % 2].after(i, 16 * (n // 2)))
                    act.wait_ge(*banks.full(i, ("M", a, g)))
                    act.activation(negmax[:, n % 2, :], banks.bank(("M", a, g))[0:GH * TT, 0:P], ACT.Copy,
                                   scale=-1.0).then_inc(banks.release(("M", a, g)), 1)
                    act.wait_ge(*banks.out(i, ("M", a, g)))
                    act.sem_inc(act_turn, 1)
                    act.dma_start(stacks[n % STACKS][ROWMAX:ROWMAX + 1, 0, :, :].rearrange("o h t -> o (h t)")
                                  .bitcast(F32), negmax[:, n % 2, :].bitcast(F32)).then_inc(negmax_in[n % 2].sem, 16)

                def exps(i, a, g, j, h):
                    m = (a * NG + g) * TT + j
                    if h == 0:
                        act.wait_ge(*pv_done.after(i, max(0, m - 1)))
                    first, width = (P, P) if j == TT - 1 else (0, T - P * j)
                    u = GH * m + h
                    act.wait_ge(*st_filled.after(i, u + 1))
                    act.activation(probs[:, m % 2, h, 0:width], scoresT[:, u % 3, first:first + width],
                                   ACT.Exp, scale=SCALE).then_inc(exp_done.sem, 1)

                def take_output(i, a, g):
                    n = a * NG + g
                    act.wait_ge(*out_done.after(i, TT * n))
                    act.wait_ge(*pv_done.after(i, TT * (n + 1)))
                    act.activation(total[:, :], sum_ps[:, :], ACT.Copy)
                    act.activation(whole[:, :], out_ps[:, :], ACT.Copy).then_inc(taken.sem, 1)

                def norm(i, kind, t):
                    if kind == "A":
                        act.wait_ge(*shift_done[0].after(i, t + 1))
                        act.activation(v[:, t, :], banks.bank(("y", 0, t)), ACT.Identity,
                                       bias=shift[:, 0, t, 0:1], scale=rstd[:, 1, t, 0:1])\
                           .then_inc(banks.release(("y", 0, t)), 1)
                    if kind == "C":
                        act.wait_ge(*shift_done[1].after(i, t + 1))
                        act.activation(v[:, t, :], x1[:, t, :], ACT.Identity,
                                       bias=shift[:, 1, t, 1:2], scale=rstd[:, 2, t, 1:2]).then_inc(xr_done.sem, 1)
                    if kind == "D":
                        act.activation(xin[:, t, :], x1[:, t, :], ACT.Identity,
                                       bias=shift[:, 1, t, 0:1], scale=rstd[:, 2, t, 0:1]).then_inc(xin_done.sem, 1)

                def attend(i, a):
                    for step, *which in attention_order(a):
                        if step == "O":
                            take_output(i, a, *which)
                        if step == "T":
                            take_high(i, a, *which)
                        if step == "V":
                            t = which[0]
                            if a == 0 and t == 0:
                                act.wait_ge(*h_stored.after(i, 0))
                            copy(i, ("v", a, t), v[:, t, :])
                        if step == "M":
                            take_negmax(i, a, *which)
                        if step == "ST":
                            exps(i, a, *which)
                        if step == "Y" and which[1] == 1 and a == 0:
                            for kind, t in norm_order(which[0]):
                                norm(i, kind, t)

                act.wait_ge(rest_in, 16 * N_REST)
                act.wait_ge(consts, N_CONSTS)
                with act.Fori(0, blocks) as i:
                    for c in range(CT):
                        copy(i, ("xT", c), xT[:, c, :])
                    attend(i, 0)
                    for c in range(CT):
                        copy(i, ("xrT", c), xT[:, c, :], scale=ln1w[:, c:c + 1])
                    for m in range(2):
                        copy(i, ("lat", m), latT[:, m, :])
                    attend(i, 1)

            @block.vector
            def _(dve):
                for n in range(STACKS):
                    dve.memset(stacks[n][ROWMAX:ROWMAX + 1, 1, :, :].bitcast(F32), 1.0).then_inc(consts, 1)
                dve.wait_ge(consts, N_CONSTS)

                def take_stats(i, m, t, rows, before=0):
                    dve.bn_stats(stats[:, m, t, :], rows).then_inc(stats_done[m].sem, 1)
                    dve.wait_ge(*stats_done[m].after(i, before + t + 1))
                    dve.sem_inc(dve_turn, 1)
                    dve.bn_aggr(meanvar[:, m, t, :], stats[:, m, t, :]).then_inc(meanvar_done[m].sem, 1)

                def norm(to, rows, m, t, s, done):
                    dve.tensor_scalar(to[:, t, :], rows[:, t, :], meanvar[:, m, t, 0:1], rstd[:, m, t, s:s + 1],
                                      ALU.subtract, ALU.mult).then_inc(done.sem, 1)

                def rotate(i, a, g, which):
                    r = 2 * (a * NG + g) + which
                    name = ("q", "k")[which], a, g
                    dve.wait_ge(*banks.full(i, name))
                    if a == 0:
                        rows = banks.bank(name).rearrange("p (t h d) -> p t h d", t=TT, h=GH)
                    else:
                        split = "p (t h s d) -> p t h s d" if which == 0 else "p (t s h d) -> p t h s d"
                        halves = banks.bank(name).rearrange(split, t=TT, h=GH, s=2)
                        to = qk[:, g % 2, which, :, :].rearrange("p t (h s d) -> p t h s d", h=GH, s=2)
                        if g >= 2:
                            dve.sem_inc(dve_turn, 1)
                            dve.wait_ge(*banks.full(i, ("kT", a, g - 2)))
                        dve.tensor_copy(to[:, :, :, 0, :], halves[:, :, :, 0, :]).then_inc(plain_done.sem, 1)
                        rows = halves[:, :, :, 1, :]
                    dve.wait_ge(*rotated.after(i, max(0, r - 1)))
                    width, table = ((HD, rope1), (RD, rope2))[a]
                    cos_part, sin_part = (turned[:, r % 2, s, 0:TT * GH * width]
                                          .rearrange("p (t h d) -> p t h d", t=TT, h=GH) for s in range(2))
                    cos, sin = (table[:, :, s, :].unsqueeze(2).to_broadcast([P, TT, GH, width]) for s in range(2))
                    dve.tensor_tensor(cos_part, rows, cos, ALU.mult).then_inc(cos_done.sem, 1)
                    first, second = slice(0, width // 2), slice(width // 2, width)
                    dve.tensor_tensor(sin_part[:, :, :, first], rows[:, :, :, second], sin[:, :, :, first], ALU.mult)
                    dve.tensor_tensor(sin_part[:, :, :, second], rows[:, :, :, first], sin[:, :, :, second], ALU.mult)\
                       .then_inc(banks.release(name), 1)

                def take_low(i, a, g):
                    n = a * NG + g
                    for which, name in enumerate(("qT", "kT")):
                        dve.wait_ge(*high_done.after(i, 2 * n + which + 1))
                        dve.tensor_tensor(parts[:, 2 + which, :], banks.bank((name, a, g)), parts[:, which, :],
                                          ALU.subtract).then_inc(banks.release((name, a, g)), 1)

                def maxima(i, a, g, h):
                    n = a * NG + g
                    before = divmod(GH * n + h - 1, GH)
                    for t in range(TT):
                        name = ("S", a, g, h, max(0, t - 1))
                        first = P * 2 * (t == 1)
                        dve.wait_ge(*banks.full(i, name))
                        if t == 0 or before[0] < 0:
                            dve.wait_ge(*max_done.after(i, GH * n + h))
                        else:
                            dve.wait_ge(*banks.out(i, ("S", *divmod(before[0], NG), before[1], t - 1)))
                        dve.sem_inc(dve_turn, 1)
                        width = P * (t + 1)
                        ins = dve.tensor_tensor_reduce(
                            unused[:, t, 0:width], banks.bank(name)[:, first:first + width],
                            mask[:, T - width:T], 1.0, MASKED, ALU.add, ALU.max,
                            rowmax[:, n % 2, TT * h + t:TT * h + t + 1])
                        if t == 0:
                            ins.then_inc(max_done.sem, 1)
                        else:
                            ins.then_inc(banks.release(name), 1)

                def close(i, a, g, t):
                    m = (a * NG + g) * TT + t
                    mine = slice(t * P, (t + 1) * P)
                    dve.wait_ge(*taken.after(i, a * NG + g + 1))
                    dve.reciprocal(total[:, mine], total[:, mine]).then_inc(total_done.sem, 1)
                    dve.wait_ge(*total_done.after(i, m + 1))
                    dve.tensor_tensor(outT[:, g, mine], whole[:, mine], total[:, mine], ALU.mult)\
                       .then_inc(out_done.sem, 1)

                def norm_step(i, step, t):
                    if step == "A":
                        dve.wait_ge(*banks.full(i, ("y", 0, t)))
                        dve.sem_inc(dve_turn, 1)
                        take_stats(i, 1, t, banks.bank(("y", 0, t)))
                    if step == "B":
                        dve.wait_ge(*banks.out(i, ("y", 0, t)))
                        dve.tensor_tensor(x1[:, t, :], v[:, t, :], x_in[:, t, :], ALU.add)\
                           .then_inc(x1_done.sem, 1)
                        dve.wait_ge(*x1_done.after(i, t + 1))
                        take_stats(i, 2, t, x1[:, t, :])

                def attend(i, a):
                    for step, *which in attention_order(a):
                        if step == "P":
                            rotate(i, a, *which)
                        if step == "T":
                            take_low(i, a, *which)
                        if step == "S":
                            g, h = which
                            if h == 0 and g >= 2:
                                dve.wait_ge(*banks.full(i, ("M", a, g - 2)))
                                dve.sem_inc(dve_turn, 1)
                            maxima(i, a, g, h)
                        if step == "C":
                            close(i, a, *which)
                        if step == "Y" and which[1] == 1:
                            t = which[0]
                            if a == 0:
                                for of in norm_order(t):
                                    norm_step(i, *of)
                            else:
                                if t == 0:
                                    dve.wait_ge(*xin_done.after(i, TT))
                                dve.wait_ge(*banks.full(i, ("y", 1, t)))
                                dve.tensor_tensor(v[:, t, :], banks.bank(("y", 1, t)), xin[:, t, :], ALU.add)\
                                   .then_inc(banks.release(("y", 1, t)), 1)
                        if step == "L":
                            dve.wait_ge(*x_loaded.after(i, 32))
                            take_stats(i, 0, which[0], x_in[:, which[0], :], before=TT)
                        if step == "N":
                            dve.wait_ge(*rstd_done[0].after(i, 2))
                            dve.wait_ge(*x1_stored.after(i, 16))
                            dve.wait_ge(*xin_done.after(i, TT))
                            norm(x1, x_in, 0, which[0], 0, first_normed)

                dve.wait_ge(*x_loaded.after(0, 16))
                for t in range(TT):
                    take_stats(0, 0, t, x_in[:, t, :])
                dve.wait_ge(*rstd_done[0].after(0, 1))
                for t in range(TT):
                    norm(x1, x_in, 0, t, 0, first_normed)
                dve.wait_ge(qkv_in, 32)
                dve.wait_ge(rest_in, 16 * N_REST)
                with dve.Fori(0, blocks) as i:
                    attend(i, 0)
                    attend(i, 1)

            @block.tensor
            def _(pe):

                def product(to, pairs):
                    for n, (left, right) in enumerate(pairs):
                        ins = pe.matmul(to, left, right, start=(n == 0), stop=(n == len(pairs) - 1))
                    return ins

                def tile_of(rows_T, c, t):
                    return rows_T[:, c, t * P:(t + 1) * P]

                def transpose_columns(i, name, rows, c):
                    pe.wait_ge(*banks.empty(i, name))
                    for t in range(TT):
                        ins = pe.transpose(tile_of(ring, banks.at(name), t), rows[:, t, c * P:(c + 1) * P], ident[:, :])
                    ins.then_inc(filled, 1)

                def project(i, a, g, which):
                    name = ("q", "k")[which], a, g
                    pe.wait_ge(*banks.empty(i, name))
                    for t in range(TT):
                        to = tile_of(ring, banks.at(name), t)
                        if a == 0:
                            first = which * D + g * P
                            ins = product(to, [(tile_of(xT, c, t), wqkv[:, c, first:first + P]) for c in range(CT)])
                        elif which == 0:
                            ins = product(to, [(tile_of(latT, 1, t),
                                                wq2[:, g * GH:(g + 1) * GH, :, :].rearrange("p h s d -> p (h s d)"))])
                        else:
                            mine = slice(g * GH * RD, (g + 1) * GH * RD)
                            product(to[:, 0:GH * RD], [(tile_of(latT, 0, t), wku[:, mine])])
                            ins = product(to[:, GH * RD:P], [(tile_of(xT, c, t), wkr[:, c, mine]) for c in range(CT)])
                    ins.then_inc(filled, 1)

                def transpose_group(i, a, g):
                    n = a * NG + g
                    for which, name in enumerate(("qT", "kT")):
                        pe.wait_ge(*banks.empty(i, (name, a, g)))
                        pe.wait_ge(*rotated.after(i, 2 * n + which + 1))
                        if a == 1:
                            pe.wait_ge(*plain_done.after(i, 2 * g + which + 1))
                        for t in range(TT):
                            ins = pe.transpose(tile_of(ring, banks.at((name, a, g)), t),
                                               qk[:, g % 2, which, t, :], ident[:, :])
                        ins.then_inc(filled, 1)

                def values(i, a, t):
                    name = "v", a, t
                    pe.wait_ge(*banks.empty(i, name))
                    if a == 0:
                        pairs = [(tile_of(xT, c, t), wqkv[:, c, 2 * D:3 * D]) for c in range(CT)]
                    else:
                        pairs = [(tile_of(latT, 0, t), wvu[:, :])]
                    product(banks.bank(name), pairs).then_inc(filled, 1)

                def scores(i, a, g, h):
                    n = a * NG + g
                    heads = stacks[n % STACKS]
                    pe.wait_ge(*stacked[n][h].after(i, PER_STACK))
                    for part, tiles in enumerate(((0, 1), (2,), (3,))):
                        name = "S", a, g, h, part
                        pe.wait_ge(*banks.empty(i, name))
                        for t in tiles:
                            width = max(2 * P, P * (t + 1))
                            first = 2 * P * (t == 1)
                            ins = pe.matmul(banks.bank(name)[:, first:first + width],
                                            heads[0:ROWMAX, 0, h, t * P:(t + 1) * P],
                                            heads[0:ROWMAX, 1, h, 0:width], start=True, stop=True)
                        ins.then_inc(filled, 1)

                def transpose_max(i, a, g):
                    n = a * NG + g
                    name = "M", a, g
                    pe.wait_ge(*banks.empty(i, name))
                    pe.wait_ge(*max_done.after(i, GH * (n + 1)))
                    last = "S", a, g, GH - 1, 2
                    if banks.at(last) != banks.at(name):
                        pe.wait_ge(*banks.out(i, last))
                    pe.transpose(banks.bank(name)[0:GH * TT, 0:P], rowmax[:, n % 2, :], ident[:, :]).then_inc(filled, 1)

                def scores_less_max(i, a, g, j, h):
                    n = a * NG + g
                    heads = stacks[n % STACKS]
                    if j == 0 and h == 0:
                        pe.wait_ge(*negmax_in[n % 2].after(i, 16 * (n // 2 + 1)))
                    first = min(P * j, T - 2 * P)
                    u = GH * (TT * n + j) + h
                    pe.wait_ge(*exp_done.after(i, max(0, u - 2)))
                    pe.matmul(scoresT[:, u % 3, 0:T - first], heads[0:ROWMAX + 1, 1, h, j * P:(j + 1) * P],
                              heads[0:ROWMAX + 1, 0, h, first:T], start=True, stop=True).then_inc(st_filled.sem, 1)

                def times_v(i, a, g, j):
                    n = a * NG + g
                    m = TT * n + j
                    if j == 0:
                        pe.wait_ge(*taken.after(i, n))
                    if g == 0:
                        pe.wait_ge(*banks.out(i, ("v", a, j)))
                    pe.wait_ge(*causal.after(i, m + 1))
                    for to, is_sum in ((out_ps, False), (sum_ps, True)):
                        for h in range(GH):
                            head = (GH * g + h) * HD
                            left = ones[:, :] if is_sum else v[:, j, head:head + HD]
                            ins = pe.matmul(to[h * HD:(h + 1) * HD, P * j:T], left,
                                            probs[:, m % 2, h, 0:T - P * j],
                                            start=(j == 0), stop=(j == TT - 1))
                    ins.then_inc(pv_done.sem, 1)

                def output(i, a, t, last):
                    name = "y", a, t
                    if not last:
                        pe.wait_ge(*banks.empty(i, name))
                        pe.wait_ge(*out_done.after(i, TT * (a * NG + NG - 1)))
                    else:
                        pe.wait_ge(*out_done.after(i, TT * (a * NG + NG - 1) + t + 1))
                    for c in ([CT - 1] if last else range(CT - 1)):
                        ins = pe.matmul(banks.bank(name), tile_of(outT, c, t), wo[:, a, c, :],
                                        start=(c == 0), stop=(c == CT - 1))
                    if last:
                        ins.then_inc(filled, 1)

                def attend(i, a):
                    for step, *which in attention_order(a):
                        if step == "P":
                            project(i, a, *which)
                        if step == "T":
                            transpose_group(i, a, *which)
                        if step == "V":
                            values(i, a, *which)
                        if step == "S":
                            scores(i, a, *which)
                        if step == "M":
                            transpose_max(i, a, *which)
                        if step == "ST":
                            scores_less_max(i, a, *which)
                        if step == "PV":
                            times_v(i, a, *which)
                        if step == "Y":
                            output(i, a, *which)

                pe.wait_ge(consts, N_CONSTS)
                pe.wait_ge(qkv_in, 32)
                pe.wait_ge(rest_in, 16 * N_REST)
                with pe.Fori(0, blocks) as i:
                    pe.wait_ge(*first_normed.after(i, TT))
                    for c in range(CT):
                        transpose_columns(i, ("xT", c), x1, c)
                    pe.wait_ge(*banks.out(i, ("xT", CT - 1)))
                    attend(i, 0)
                    pe.wait_ge(*xr_done.after(i, TT))
                    for c in range(CT):
                        transpose_columns(i, ("xrT", c), v, c)
                    pe.wait_ge(*banks.out(i, ("xrT", CT - 1)))
                    for m in range(2):
                        pe.wait_ge(*banks.empty(i, ("lat", m)))
                        product(banks.bank(("lat", m)), [(wlat[:, c, m, :], xT[:, c, :]) for c in range(CT)])\
                            .then_inc(filled, 1)
                    pe.wait_ge(*banks.out(i, ("lat", 1)))
                    attend(i, 1)


def norm_order(last):
    yield "A", last
    if last >= 1:
        yield "B", last - 1
    if last >= 2:
        yield "C", last - 2
    if last == TT - 1:
        yield from [("B", last), ("C", last - 1), ("C", last), *(("D", t) for t in range(TT))]


def expert_layer(nc, h_in, x1_in, ln2_w, weights, out, blocks):
    gates, ups, downs, router_w, router_b = weights
    parts = blocks // NB
    with ExitStack() as ctx:
        signals = []

        def sb(name, shape, dt=F32):
            return ctx.enter_context(nc.sbuf_tensor(name, shape, dt))

        def semaphore(name):
            return ctx.enter_context(nc.semaphore(name))

        def signal(name, per_pass):
            signals.append(Signal(semaphore(name), per_pass))
            return signals[-1]

        raw = sb("raw", [P, 3, WIDE])
        wh = sb("wh", [P, 2, 3, WIDE], F32R)
        wl = sb("wl", [P, 2, 3, WIDE], F32R)
        wr = sb("wr", [P, CT, NR])
        wrh = sb("wrh", [P, CT, NR], F32R)
        wrl = sb("wrl", [P, CT, NR], F32R)
        rb = sb("rb", [NR, 1])
        ln2w = sb("ln2w", [P, CT])
        ident = sb("ident2", [P, P])
        number = sb("number", [P, NR])
        minus_half = sb("minus_half2", [P, TT])
        h = sb("h", [P, NB, TT, D])
        xh = sb("xh", [P, NB, CT, T], F32R)
        xl = sb("xl", [P, NB, CT, T], F32R)
        x1 = sb("x1b", [P, 2, TT, D])
        xr = sb("xr", [P, TT, D])
        tanh = sb("tanh", [P, FT, T])
        gated = sb("gated", [P, FT, T])
        acts = sb("acts", [P, FT, T])
        acth = sb("acth", [P, FT, T], F32R)
        actl = sb("actl", [P, FT, T], F32R)
        zT = sb("zT", [P, T])
        half = sb("half", [P, TT, NR])
        chance = sb("chance", [P, TT, 8])
        best = sb("best", [P, TT, 8])
        where = sb("where", [P, TT, 8], U32)
        wheref = sb("wheref", [P, TT, 2])
        den = sb("den", [P, TT])
        rden = sb("rden", [P, TT])
        share = sb("share", [P, TT, 2])
        part = sb("part", [P, 2, TT, NR])
        gain = sb("gain", [P, 2, NB, TT, NE])
        square = sb("square", [P, TT])
        padded = sb("padded2", [P, 2, TT])
        rms = sb("rms_h", [P, TT])
        stats = sb("stats2", [P, TT, 6])
        meanvar = sb("meanvar2", [P, TT, 2])
        rstd = sb("rstd2", [P, TT])

        def ring(name, n, names):
            tensor = ctx.enter_context(nc.psum_tensor(name, [P, n, 512], F32))
            made = Banks(tensor, semaphore(f"{name}_filled"), [semaphore(f"{name}_freed{k}") for k in range(n)], names)
            rings.append(made)
            return made

        rings = []
        UNITS = 2 * NB
        into = ring("into", 2, [(kind, u, m) for u in range(UNITS) for m in range(FT) for kind in ("gate", "up")])
        down = ring("down", TT, [(u, t) for u in range(UNITS) for t in range(TT)])
        opening = ring("opening", 2, [(b, *of) for b in range(NB)
                                      for of in (*(("xT", c) for c in range(CT)), ("z", 0), ("zT", 0))])

        small_in = semaphore("small_in")
        N_SMALL, N_CONSTS = 3, 6
        consts = semaphore("consts2")
        consts_step = semaphore("consts2_step")
        pool_turn, dve_turn, sp_turn, pe_turn = (semaphore(f"{e}_turn2") for e in ("pool", "dve", "sp", "pe"))
        raw_in = signal("raw_in", 2 * 48)
        split_high = signal("split_high", 2 * CHUNKS)
        split_low = signal("split_low", 2 * CHUNKS)
        tanh_done = signal("tanh_done", UNITS * FT)
        act_high = signal("act_high", UNITS * FT)
        act_low = signal("act_low", UNITS * FT)
        shifted = signal("shifted", UNITS)
        h_loaded = [Signal(semaphore(f"h_loaded{b}"), 16, start=0) for b in range(NB)]
        squared = signal("squared", NB * TT)
        padded_done = signal("padded2_done", 2 * NB)
        rms_done = signal("rms_done", NB)
        xr_done = signal("xr_done2", NB * TT)
        x_high = signal("x_high", NB * CT)
        ROUTE = 4 * TT + 7
        route_step = signal("route_step", NB * ROUTE)
        x1_loaded = [signal(f"x1_loaded{n}", NB // 2 * 16) for n in range(2)]
        stored = [signal(f"stored{n}", NB // 2 * 16) for n in range(2)]
        stats_done = signal("stats2_done", NB * TT)
        meanvar_done = signal("meanvar2_done", NB * TT)
        rstd_done = signal("rstd2_done", NB)
        closed = signal("closed", NB * TT)
        out_ready = [signal(f"out_ready{b}", TT) for b in range(NB)]

        with nc.Block() as block:
            @block.sync
            def _(sp):
                for s in signals:
                    sp.sem_inc(s.sem, 1)
                for made in rings:
                    for sem in [made.filled, *made.freed]:
                        sp.sem_inc(sem, 1)

        with nc.Block() as block:

            @block.sync
            def _(sp):
                in_rows = "o (t p) c -> p (o t) c"

                def load_expert(e):
                    for n, of in enumerate((gates, ups, downs)):
                        width = of.shape[-1]
                        sp.dma_start(raw[:, n, :].rearrange("p (c n) -> p c n", n=width),
                                     of[bass.ds(e, 1), :, :].rearrange("o (c p) n -> p (o c) n", p=P))\
                          .then_inc(raw_in.sem, 16)

                def load_next(it, s, e):
                    sp.wait_ge(*split_high.after(it, CHUNKS * (s + 2) + 1))
                    sp.sem_inc(sp_turn, 1)
                    sp.wait_ge(*split_low.after(it, CHUNKS * (s + 2) + 1))
                    sp.sem_inc(sp_turn, 1)
                    load_expert(e)

                def load_x1(p, b):
                    sp.wait_ge(*stored[b % 2].after(p, 16 * (b // 2)))
                    sp.sem_inc(sp_turn, 1)
                    sp.dma_start(x1[:, b % 2], x1_in[bass.ds(p * NB + b, 1), :, :].rearrange(in_rows, p=P))\
                      .then_inc(x1_loaded[b % 2].sem, 16)

                def store(p, b):
                    sp.wait_ge(*out_ready[b].after(p, TT))
                    sp.sem_inc(sp_turn, 1)
                    sp.dma_start(out[bass.ds(p * NB + b, 1), :, :].rearrange(in_rows, p=P), x1[:, b % 2])\
                      .then_inc(stored[b % 2].sem, 16)

                sp.dma_start(ln2w[:, :], ln2_w).then_inc(small_in, 16)
                sp.dma_start(wr[:, :, :], router_w.rearrange("(c p) n -> p c n", p=P)).then_inc(small_in, 16)
                sp.dma_start(rb[:, :], router_b).then_inc(small_in, 16)
                load_expert(0)
                sp.wait_ge(*split_high.after(0, CHUNKS + 1))
                sp.wait_ge(*split_low.after(0, CHUNKS + 1))
                load_expert(1)
                with sp.Fori(0, parts) as p:
                    for s in range(2):
                        load_next(p * PAIRS, s, 2 + s)
                    with sp.Fori(p * PAIRS + 1, p * PAIRS + PAIRS - 1) as it:
                        for s in range(2):
                            load_next(it, s, (it + 1) % PAIRS * 2 + s)
                    last = p * PAIRS + PAIRS - 1
                    load_x1(p, 0)
                    load_x1(p, 1)
                    load_next(last, 0, 0)
                    store(p, 0)
                    load_x1(p, 2)
                    store(p, 1)
                    load_x1(p, 3)
                    load_next(last, 1, 1)
                    store(p, 2)
                    store(p, 3)
                for n in range(2):
                    sp.wait_ge(*stored[n].after(parts - 1, NB // 2 * 16))
                sp.wait_ge(*raw_in.after(parts * PAIRS - 1, 4 * 48))

            @block.gpsimd
            def _(pool):
                pool.memset(ident[:, :], 0.0).then_inc(consts_step, 1)
                pool.memset(zT[:, :], 0.0).then_inc(consts, 1)
                pool.memset(minus_half[:, :], -0.5).then_inc(consts, 1)
                pool.memset(chance[:, :, :], -1.0).then_inc(consts, 1)
                pool.iota(number[:, :], pattern=[[1, NR]], base=0, channel_multiplier=0,
                          allow_small_or_imprecise_dtypes=True).then_inc(consts, 1)
                pool.wait_ge(consts_step, 1)
                pool.affine_select(out=ident[:, :], in_=ident[:, :], compare_op=ALU.not_equal, fill=1.0,
                                   base=0, pattern=[[-1, P]], channel_multiplier=1).then_inc(consts, 1)
                with pool.Fori(0, parts) as p:
                    for b in range(NB):
                        pool.wait_ge(*out_ready[b].after(p, 0))
                        pool.sem_inc(pool_turn, 1)
                        pool.dma_start(h[:, b], h_in[bass.ds(p * NB + b, 1), :, :]
                                       .rearrange("o (t p) c -> p (o t) c", p=P)).then_inc(h_loaded[b].sem, 16)
                    for b in range(NB):
                        pool.wait_ge(*squared.after(p, TT * (b + 1)))
                        pool.sem_inc(pool_turn, 1)
                        pool.tensor_scalar(padded[:, 0, :], square[:, :], EPS, None, ALU.add)\
                            .then_inc(padded_done.sem, 1)
                        pool.wait_ge(*padded_done.after(p, b + 1))
                        pool.wait_ge(*xr_done.after(p, TT * b))
                        pool.tensor_tensor(rms[:, :], padded[:, 0, :], minus_half[:, :], ALU.pow)\
                            .then_inc(rms_done.sem, 1)
                    for b in range(NB):
                        pool.wait_ge(*meanvar_done.after(p, TT * (b + 1)))
                        pool.sem_inc(pool_turn, 1)
                        pool.tensor_scalar(padded[:, 1, :], meanvar[:, :, 1], EPS, None, ALU.add)\
                            .then_inc(padded_done.sem, 1)
                        pool.wait_ge(*padded_done.after(p, NB + b + 1))
                        pool.tensor_tensor(rstd[:, :], padded[:, 1, :], minus_half[:, :], ALU.pow)\
                            .then_inc(rstd_done.sem, 1)

            @block.scalar
            def _(act):

                def split(k, buffer):
                    n, half_of = divmod(k, 2)
                    mine = slice(half_of * 512, half_of * 512 + 512)
                    act.activation(wh[:, buffer, n, mine], raw[:, n, mine], ACT.Copy).then_inc(split_high.sem, 1)

                def normed(p, b):
                    act.wait_ge(*rms_done.after(p, b + 1))
                    for t in range(TT):
                        act.activation(xr[:, t, :], h[:, b, t, :], ACT.Copy, scale=rms[:, t:t + 1])\
                           .then_inc(xr_done.sem, 1)

                def high_rows(p, b, c):
                    name = b, "xT", c
                    act.wait_ge(*opening.full(p, name))
                    act.activation(xh[:, b, c, :], opening.bank(name), ACT.Copy, scale=ln2w[:, c:c + 1])\
                       .then_inc(x_high.sem, 1)

                def logits(p, b):
                    act.wait_ge(*opening.full(p, (b, "z", 0)))
                    act.activation(zT[0:NR, :], opening.bank((b, "z", 0))[0:NR, :], ACT.Identity, bias=rb[:, 0:1])\
                       .then_inc(opening.release((b, "z", 0)), 1)

                def chances(p, b):
                    act.wait_ge(*opening.full(p, (b, "zT", 0)))
                    act.activation(half[:, :, :],
                                   opening.bank((b, "zT", 0)).rearrange("p (t n) -> p t n", t=TT)[:, :, 0:NR],
                                   ACT.Tanh, scale=0.5).then_inc(opening.release((b, "zT", 0)), 1)

                def pair(p, it, kind):
                    for u in range(UNITS):
                        s, b = divmod(u, NB)
                        opened = b + 1 if kind == "first" and s == 0 and b + 1 < NB else None
                        for m in range(FT):
                            if opened is not None:
                                high_rows(p, opened, 2 * m)
                            act.wait_ge(*into.full(it, ("gate", u, m)))
                            act.activation(tanh[:, m, :], into.bank(("gate", u, m)), ACT.Tanh, scale=0.5)\
                               .then_inc(tanh_done.sem, 1)
                            if m == 0:
                                for k in CHUNKS_IN.get(b, ()):
                                    act.wait_ge(*raw_in.after(it, 48 * (s + 2)))
                                    split(k, 1 - s)
                            if opened is not None:
                                high_rows(p, opened, 2 * m + 1)
                            act.wait_ge(*into.out(it, ("up", u, m)))
                            act.activation(acth[:, m, :], acts[:, m, :], ACT.Copy).then_inc(act_high.sem, 1)
                        if opened is not None:
                            logits(p, opened)
                            chances(p, opened)
                            if opened + 1 < NB:
                                normed(p, opened + 1)

                act.wait_ge(consts, N_CONSTS)
                act.wait_ge(small_in, 16 * N_SMALL)
                act.activation(wrh[:, :, :], wr[:, :, :], ACT.Copy).then_inc(split_high.sem, 1)
                act.wait_ge(*raw_in.after(0, 48))
                for k in range(CHUNKS):
                    split(k, 0)
                with act.Fori(0, parts) as p:
                    normed(p, 0)
                    for c in range(CT):
                        high_rows(p, 0, c)
                    logits(p, 0)
                    chances(p, 0)
                    normed(p, 1)
                    pair(p, p * PAIRS, "first")
                    with act.Fori(p * PAIRS + 1, p * PAIRS + PAIRS - 1) as it:
                        pair(p, it, "middle")
                    pair(p, p * PAIRS + PAIRS - 1, "last")

            @block.vector
            def _(dve):
                dve.memset(gain[:, :, :, :, :], 0.0).then_inc(consts, 1)
                dve.wait_ge(consts, N_CONSTS)
                dve.wait_ge(small_in, 16 * N_SMALL)

                def split(k, buffer):
                    n, half_of = divmod(k, 2)
                    mine = slice(half_of * 512, half_of * 512 + 512)
                    dve.tensor_tensor(wl[:, buffer, n, mine], raw[:, n, mine], wh[:, buffer, n, mine], ALU.subtract)\
                       .then_inc(split_low.sem, 1)

                def squares(p, b):
                    dve.wait_ge(*h_loaded[b].after(p, 16))
                    dve.wait_ge(*rms_done.after(p, b))
                    dve.sem_inc(dve_turn, 1)
                    if b > 0:
                        dve.wait_ge(*opening.full(p, (b - 1, "xT", CT - 1)))
                        dve.sem_inc(dve_turn, 1)
                    for t in range(TT):
                        dve.tensor_tensor_reduce(xr[:, t, :], h[:, b, t, :], h[:, b, t, :], 1.0 / D, 0.0,
                                                 ALU.mult, ALU.add, square[:, t:t + 1]).then_inc(squared.sem, 1)

                def low_rows(p, b, c):
                    name = b, "xT", c
                    dve.wait_ge(*x_high.after(p, CT * b + c + 1))
                    dve.scalar_tensor_tensor(out=xl[:, b, c, :], in0=opening.bank(name), scalar=ln2w[:, c:c + 1],
                                             in1=xh[:, b, c, :], op0=ALU.mult, op1=ALU.subtract)\
                       .then_inc(opening.release(name), 1)

                def routing(p, b):
                    done = b * ROUTE
                    dve.wait_ge(*opening.out(p, (b, "zT", 0)))
                    dve.tensor_scalar(chance[:, :, 0:NR], half[:, :, :], 0.5, 0.5, ALU.mult, ALU.add)\
                       .then_inc(route_step.sem, 1)
                    done += 1
                    dve.wait_ge(*route_step.after(p, done))
                    dve.sem_inc(dve_turn, 1)
                    for t in range(TT):
                        dve.max(best[:, t, :], chance[:, t, :]).then_inc(route_step.sem, 1)
                    done += TT
                    dve.wait_ge(*route_step.after(p, done))
                    dve.sem_inc(dve_turn, 1)
                    for t in range(TT):
                        dve.max_index(where[:, t, :], best[:, t, :], chance[:, t, :]).then_inc(route_step.sem, 1)
                    dve.tensor_tensor(den[:, :], best[:, :, 0], best[:, :, 1], ALU.add).then_inc(route_step.sem, 1)
                    done += TT + 1
                    dve.wait_ge(*route_step.after(p, done))
                    dve.reciprocal(rden[:, :], den[:, :]).then_inc(route_step.sem, 1)
                    dve.tensor_copy(wheref[:, :, :], where[:, :, 0:2]).then_inc(route_step.sem, 1)
                    done += 2
                    dve.wait_ge(*route_step.after(p, done))
                    dve.tensor_tensor(share[:, :, :], best[:, :, 0:2],
                                      rden[:, :].unsqueeze(2).to_broadcast([P, TT, 2]), ALU.mult)\
                       .then_inc(route_step.sem, 1)
                    done += 1
                    dve.wait_ge(*route_step.after(p, done))
                    for s in range(2):
                        for t in range(TT):
                            dve.tensor_scalar(part[:, s, t, :], number[:, :], wheref[:, t, s:s + 1],
                                              share[:, t, s:s + 1], ALU.is_equal, ALU.mult)\
                               .then_inc(route_step.sem, 1)
                    done += 2 * TT
                    dve.wait_ge(*route_step.after(p, done))
                    dve.tensor_tensor(gain[:, 0, b, :, 1:NE], part[:, 0], part[:, 1], ALU.add)\
                       .then_inc(route_step.sem, 1)
                    dve.memset(gain[:, 0, b, :, 0:1], 1.0).then_inc(route_step.sem, 1)
                    assert done + 2 == (b + 1) * ROUTE

                def activate(it, u, m):
                    k = u * FT + m
                    dve.wait_ge(*tanh_done.after(it, k + 1))
                    dve.scalar_tensor_tensor(out=gated[:, m, :], in0=tanh[:, m, :], scalar=1.0,
                                             in1=into.bank(("gate", u, m)), op0=ALU.add, op1=ALU.mult)\
                       .then_inc(into.release(("gate", u, m)), 1)
                    dve.wait_ge(*into.out(it, ("gate", u, m)))
                    dve.wait_ge(*into.full(it, ("up", u, m)))
                    dve.scalar_tensor_tensor(out=acts[:, m, :], in0=gated[:, m, :], scalar=1.0 / 16.0,
                                             in1=into.bank(("up", u, m)), op0=ALU.mult, op1=ALU.mult)\
                       .then_inc(into.release(("up", u, m)), 1)
                    dve.wait_ge(*act_high.after(it, k + 1))
                    dve.tensor_tensor(actl[:, m, :], acts[:, m, :], acth[:, m, :], ALU.subtract)\
                       .then_inc(act_low.sem, 1)

                def add_expert(p, it, kind, u):
                    s, b = divmod(u, NB)
                    if kind == "first" and s == 0:
                        dve.wait_ge(*route_step.after(p, ROUTE * (b + 1)))
                    else:
                        dve.wait_ge(*shifted.after(it, u - NB + 1))
                    dve.sem_inc(dve_turn, 1)
                    for t in range(TT):
                        dve.wait_ge(*down.full(it, (u, t)))
                        dve.wait_ge(*down.empty(it, (u, t)))
                        dve.scalar_tensor_tensor(out=h[:, b, t, :], in0=down.bank((u, t)),
                                                 scalar=gain[:, s, b, t, 0:1], in1=h[:, b, t, :],
                                                 op0=ALU.mult, op1=ALU.add).then_inc(down.release((u, t)), 1)
                    dve.tensor_copy(gain[:, 1 - s, b, :, 0:NE - 1], gain[:, s, b, :, 1:NE]).then_inc(shifted.sem, 1)

                def closing_stats(p, it, b):
                    for t in range(TT):
                        dve.wait_ge(*down.out(it, (NB + b, t)))
                        dve.bn_stats(stats[:, t, :], h[:, b, t, :]).then_inc(stats_done.sem, 1)
                    for t in range(TT):
                        dve.wait_ge(*stats_done.after(p, TT * b + t + 1))
                        dve.sem_inc(dve_turn, 1)
                        dve.bn_aggr(meanvar[:, t, :], stats[:, t, :]).then_inc(meanvar_done.sem, 1)

                def close_rows(p, b):
                    dve.wait_ge(*rstd_done.after(p, b + 1))
                    for t in range(TT):
                        dve.tensor_scalar(h[:, b, t, :], h[:, b, t, :], meanvar[:, t, 0:1], rstd[:, t:t + 1],
                                          ALU.subtract, ALU.mult).then_inc(closed.sem, 1)

                def close(p, b):
                    dve.wait_ge(*x1_loaded[b % 2].after(p, 16 * (b // 2 + 1)))
                    dve.sem_inc(dve_turn, 1)
                    for t in range(TT):
                        dve.wait_ge(*closed.after(p, TT * b + t + 1))
                        dve.tensor_tensor(x1[:, b % 2, t, :], h[:, b, t, :], x1[:, b % 2, t, :], ALU.add)\
                           .then_inc(out_ready[b].sem, 1)

                def pair(p, it, kind):
                    for u in range(UNITS):
                        s, b = divmod(u, NB)
                        opened = b + 1 if kind == "first" and s == 0 and b + 1 < NB else None
                        closing = kind == "last" and s == 1
                        if opened is not None:
                            low_rows(p, opened, 0)
                            low_rows(p, opened, 1)
                        activate(it, u, 0)
                        for k in CHUNKS_IN.get(b, ()):
                            dve.wait_ge(*split_high.after(it, CHUNKS * (s + 1) + k + 2))
                            split(k, 1 - s)
                        if closing and b > 0:
                            close_rows(p, b - 1)
                        if opened is not None:
                            low_rows(p, opened, 2)
                            low_rows(p, opened, 3)
                        activate(it, u, 1)
                        if closing and b > 0:
                            close(p, b - 1)
                        if opened is not None and opened + 1 < NB:
                            squares(p, opened + 1)
                        add_expert(p, it, kind, u)
                        if opened is not None:
                            routing(p, opened)
                        if closing:
                            closing_stats(p, it, b)
                    if kind == "last":
                        close_rows(p, NB - 1)
                        close(p, NB - 1)

                dve.wait_ge(*split_high.after(0, 1))
                dve.tensor_tensor(wrl[:, :, :], wr[:, :, :], wrh[:, :, :], ALU.subtract).then_inc(split_low.sem, 1)
                for k in range(CHUNKS):
                    dve.wait_ge(*split_high.after(0, k + 2))
                    split(k, 0)
                with dve.Fori(0, parts) as p:
                    squares(p, 0)
                    for c in range(CT):
                        low_rows(p, 0, c)
                    squares(p, 1)
                    routing(p, 0)
                    pair(p, p * PAIRS, "first")
                    with dve.Fori(p * PAIRS + 1, p * PAIRS + PAIRS - 1) as it:
                        pair(p, it, "middle")
                    pair(p, p * PAIRS + PAIRS - 1, "last")

            @block.tensor
            def _(pe):

                def product(to, pairs, first=True, last=True):
                    for n, (left, right) in enumerate(pairs):
                        ins = pe.matmul(to, left, right, start=(first and n == 0), stop=(last and n == len(pairs) - 1))
                    return ins

                def three(high, low, left, right):
                    return [(high[0][left], high[1][right]), (high[0][left], low[1][right]),
                            (low[0][left], high[1][right])]

                def transposed_rows(p, b, c):
                    name = b, "xT", c
                    pe.wait_ge(*opening.empty(p, name))
                    if c == 0:
                        pe.wait_ge(*xr_done.after(p, TT * (b + 1)))
                    for t in range(TT):
                        ins = pe.transpose(opening.bank(name)[:, t * P:(t + 1) * P], xr[:, t, c * P:(c + 1) * P],
                                           ident[:, :])
                    ins.then_inc(opening.filled, 1)

                def logits(p, b):
                    name = b, "z", 0
                    pe.wait_ge(*opening.empty(p, name))
                    pe.wait_ge(*opening.out(p, (b, "xT", CT - 1)))
                    pairs = []
                    for c in range(CT):
                        pairs += three((wrh, xh), (wrl, xl), np.s_[:, c, :], np.s_[:, b, c, :])
                    product(opening.bank(name)[0:NR, :], pairs).then_inc(opening.filled, 1)

                def logits_by_token(p, b):
                    name = b, "zT", 0
                    pe.wait_ge(*opening.empty(p, name))
                    pe.wait_ge(*opening.out(p, (b, "z", 0)))
                    for t in range(TT):
                        ins = pe.transpose(opening.bank(name)[:, t * P:(t + 1) * P], zT[:, t * P:(t + 1) * P], ident[:, :])
                    ins.then_inc(opening.filled, 1)

                def pair(p, it, kind):
                    for u in range(UNITS):
                        s, b = divmod(u, NB)
                        opened = b + 1 if kind == "first" and s == 0 and b + 1 < NB else None
                        if b == 0:
                            pe.wait_ge(*split_low.after(it, CHUNKS * (s + 1) + 1))
                        for m in range(FT):
                            for n, name in enumerate(("gate", "up")):
                                pairs = []
                                for c in range(CT):
                                    first = c * FF + m * P
                                    pairs += three((wh, xh), (wl, xl), np.s_[:, s, n, first:first + P],
                                                   np.s_[:, b, c, :])
                                pe.wait_ge(*into.empty(it, (name, u, m)))
                                product(into.bank((name, u, m)), pairs).then_inc(into.filled, 1)
                                if opened is not None:
                                    transposed_rows(p, opened, 2 * m + n)
                        for m in range(FT):
                            pe.wait_ge(*act_low.after(it, u * FT + m + 1))
                            pe.sem_inc(pe_turn, 1)
                            for t in range(TT):
                                if m == 0:
                                    pe.wait_ge(*down.empty(it, (u, t)))
                                ins = product(down.bank((u, t)),
                                              three((acth, wh), (actl, wl), np.s_[:, m, t * P:(t + 1) * P],
                                                    np.s_[:, s, 2, m * D:(m + 1) * D]),
                                              first=(m == 0), last=(m == FT - 1))
                                if m == FT - 1:
                                    ins.then_inc(down.filled, 1)
                            if opened is not None:
                                (logits, logits_by_token)[m](p, opened)

                pe.wait_ge(consts, N_CONSTS)
                with pe.Fori(0, parts) as p:
                    for c in range(CT):
                        transposed_rows(p, 0, c)
                    logits(p, 0)
                    logits_by_token(p, 0)
                    pair(p, p * PAIRS, "first")
                    with pe.Fori(p * PAIRS + 1, p * PAIRS + PAIRS - 1) as it:
                        pair(p, it, "middle")
                    pair(p, p * PAIRS + PAIRS - 1, "last")


def build(nc, a, out, blocks):
    kept = [nc.dram_tensor(name, (blocks, T, D), F32, kind="Internal").ap() for name in ("x1_kept", "h_kept")]
    attention_layers(nc, a["L0_attn_x"],
                     [a[n] for n in ("L0_attn_w_qkv", "L0_attn_w_o")] +
                     [a[f"L0_ffn_{n}"] for n in ("kv_d_w", "q_d_w", "k_u_w", "v_u_w", "q_u_w", "rope_k_w",
                                                 "rope_q_w", "o_w")],
                     (a["rope1"], a["rope2"]), a["L0_ffn_ln1_w"], kept[0], kept[1], blocks)
    expert_layer(nc, kept[1], kept[0], a["L0_ffn_ln2_w"],
                 [a[n] for n in ("gates", "ups", "downs", "L0_ffn_router_w", "L0_ffn_router_b")], out, blocks)


def rope_table(width):
    inverse = (np.float32(1.0) / np.float32(10000.0) ** (np.arange(0, width, 2, dtype=np.float32) / np.float32(width)))
    angle = np.outer(np.arange(T, dtype=np.float32), inverse.astype(np.float32)).astype(np.float32)
    cos, sin = np.cos(angle), np.sin(angle)
    table = np.stack([np.concatenate([cos, cos], 1), np.concatenate([-sin, sin], 1)], 1)
    return np.ascontiguousarray(table.reshape(TT, P, 2, width).transpose(1, 0, 2, 3).astype(np.float32))


def kernel(**inputs):
    import concourse.bacc as bacc
    from concourse.bass_utils import run_bass_kernel_spmd

    nc = bacc.Bacc("TRN2", target_bir_lowering=False, num_devices=1)
    arrays, a = {}, {}
    tables = {"rope1": rope_table(HD), "rope2": rope_table(RD)}
    experts = {}
    for to, of in (("gates", "gate"), ("ups", "up"), ("downs", "down")):
        shared, routed = np.asarray(inputs.pop(f"L0_ffn_sh_{of}")), np.asarray(inputs.pop(f"L0_ffn_r_{of}"))
        experts[to] = np.concatenate([shared[None], routed])
    for name, value in {**inputs, **experts, **tables}.items():
        if name in ("L0_ffn_ln1_w", "L0_ffn_ln2_w"):
            value = np.asarray(value).reshape(CT, P).T
        if name == "L0_ffn_router_b":
            value = np.asarray(value).reshape(NR, 1)
        value = np.ascontiguousarray(value)
        arrays[f"in_{name}"] = value
        a[name] = nc.dram_tensor(f"in_{name}", value.shape, mybir.dt.from_np(value.dtype), kind="ExternalInput").ap()
    blocks = inputs["L0_attn_x"].shape[0]
    out = nc.dram_tensor("out", (blocks, T, D), F32, kind="ExternalOutput").ap()
    build(nc, a, out, blocks)
    result = run_bass_kernel_spmd(nc, [arrays], core_ids=[0])
    return result.results[0]["out"]
```
